# Optimizing a Trainium2 kernel written in Bass

```python
import numpy as np
import jax
import jax.numpy as jnp

def _softmax(x, axis=-1):
    return jax.nn.softmax(x, axis=axis)

def _gelu(x):
    return jax.nn.gelu(x, approximate=True)

def _silu(x):
    return jax.nn.silu(x)

def _sigmoid(x):
    return jax.nn.sigmoid(x)

def _layernorm(x, axis=-1, eps=1e-05):
    m = jnp.mean(x, axis=axis, keepdims=True)
    v = jnp.var(x, axis=axis, keepdims=True)
    return (x - m) / jnp.sqrt(v + eps)

def _scatter_add(tgt, idx, src, axis=0):
    return tgt.at[idx].add(src)

def _segment_sum(src, seg, n):
    return jax.ops.segment_sum(src, seg, n)
kernel_name = 'mk_vit_tower_cls_d1_tok_img256_r4_b2dc70'

def setup_inputs(seed: int=0):
    np.random.seed(seed)
    _w = jnp.asarray

    def _rec_inputs():
        import jax
        import jax.numpy as jnp
        _rk = jax.random.key(seed)
        x = -0.00016672 + 0.999947 * jax.random.normal(jax.random.fold_in(_rk, 1), (128, 3, 224, 224), jnp.float32)
        cls_tok = 0.02 * jax.random.normal(jax.random.fold_in(_rk, 5), (1, 1, 64), jnp.float32)
        return (x, cls_tok)
    x, cls_tok = _rec_inputs()

    def _L0_tok_setup():
        import jax, jax.numpy as jnp
        import numpy as np
        PATCH = 16
        key = jax.random.key(seed)
        k1, k2, k3 = jax.random.split(key, 3)
        B, C, H, Wd = (64, 3, 96, 96)
        E = 64
        pdim = PATCH * PATCH * C
        x = jax.random.normal(k1, (B, C, H, Wd), dtype=jnp.float32)
        W = jax.random.normal(k2, (E, pdim), dtype=jnp.float32) * pdim ** (-0.5)
        b = jax.random.normal(k3, (E,), dtype=jnp.float32) * 0.01
        return {'x': x, 'W': W, 'b': b}
    _L0_tok_all = _L0_tok_setup()
    _L0_tok_in = {k: v for k, v in _L0_tok_all.items() if k in ('W', 'b')}
    del _L0_tok_all

    def _L0_attn_setup():
        import jax, jax.numpy as jnp
        import numpy as np
        key = jax.random.key(seed)
        k1, k2, k3 = jax.random.split(key, 3)
        d = 64
        x = jax.random.normal(k1, (8, 512, d), dtype=jnp.float32)
        Wq = jax.random.normal(k2, (d, d), dtype=jnp.float32) * d ** (-0.5)
        Wk = jax.random.normal(k3, (d, d), dtype=jnp.float32) * d ** (-0.5)
        return {'x': x, 'Wq': Wq, 'Wk': Wk}
    _L0_attn_all = _L0_attn_setup()
    _L0_attn_in = {k: v for k, v in _L0_attn_all.items() if k in ('Wq', 'Wk')}
    del _L0_attn_all

    def _L0_ffn_setup():
        import jax, jax.numpy as jnp
        import numpy as np
        E = 8
        K = 2
        D = 64
        H = 128
        DOUT = 64
        EPS = 1e-05
        key = jax.random.key(seed)
        ks = jax.random.split(key, 9)
        s = 0.02
        return {'x': jax.random.normal(ks[0], (4, 2048, D), jnp.float32), 'gamma': 1.0 + 0.05 * jax.random.normal(ks[1], (D,), jnp.float32), 'beta': 0.05 * jax.random.normal(ks[2], (D,), jnp.float32), 'Wr': 0.01 * jax.random.normal(ks[3], (D, E), jnp.float32), 'br': jnp.zeros((E,), jnp.float32), 'W1': s * jax.random.normal(ks[4], (E, D, H), jnp.float32), 'b1': s * jax.random.normal(ks[5], (E, H), jnp.float32), 'W2': s * jax.random.normal(ks[6], (E, H, DOUT), jnp.float32), 'b2': s * jax.random.normal(ks[7], (E, DOUT), jnp.float32)}
    _L0_ffn_all = _L0_ffn_setup()
    _L0_ffn_in = {k: v for k, v in _L0_ffn_all.items() if k in ('gamma', 'beta', 'Wr', 'br', 'W1', 'b1', 'W2', 'b2')}
    del _L0_ffn_all
    return {'x': x, 'cls_tok': cls_tok, 'L0_tok_W': _L0_tok_in['W'], 'L0_tok_b': _L0_tok_in['b'], 'L0_attn_Wq': _L0_attn_in['Wq'], 'L0_attn_Wk': _L0_attn_in['Wk'], 'L0_ffn_gamma': _L0_ffn_in['gamma'], 'L0_ffn_beta': _L0_ffn_in['beta'], 'L0_ffn_Wr': _L0_ffn_in['Wr'], 'L0_ffn_br': _L0_ffn_in['br'], 'L0_ffn_W1': _L0_ffn_in['W1'], 'L0_ffn_b1': _L0_ffn_in['b1'], 'L0_ffn_W2': _L0_ffn_in['W2'], 'L0_ffn_b2': _L0_ffn_in['b2']}

def reference(x, cls_tok, L0_tok_W, L0_tok_b, L0_attn_Wq, L0_attn_Wk, L0_ffn_gamma, L0_ffn_beta, L0_ffn_Wr, L0_ffn_br, L0_ffn_W1, L0_ffn_b1, L0_ffn_W2, L0_ffn_b2):
    import jax
    import jax.numpy as jnp

    def _L0_tok_ref(x, W, b):
        import jax, jax.numpy as jnp
        import numpy as np
        PATCH = 16
        B, C, H, Wd = x.shape
        p = PATCH
        nH, nW = (H // p, Wd // p)
        patches = x.reshape(B, C, nH, p, nW, p)
        patches = patches.transpose(0, 2, 4, 1, 3, 5)
        patches = patches.reshape(B, nH * nW, C * p * p)
        return jnp.einsum('bnk,ek->bne', patches, W) + b

    def _L0_attn_ref(x, Wq, Wk):
        import jax, jax.numpy as jnp
        import numpy as np
        d = x.shape[-1]
        scale = d ** (-0.5)
        q = jnp.einsum('bnd,ed->bne', x, Wq)
        k = jnp.einsum('bnd,ed->bne', x, Wk)
        sim = jnp.einsum('bid,bjd->bij', q, k) * scale
        attn = jax.nn.softmax(sim, axis=-1)
        out = jnp.einsum('bij,bjd->bid', attn, x)
        return out

    def _L0_ffn_ref(x, gamma, beta, Wr, br, W1, b1, W2, b2):
        import jax, jax.numpy as jnp
        import numpy as np
        E = 8
        K = 2
        D = 64
        H = 128
        DOUT = 64
        EPS = 1e-05
        mu = jnp.mean(x, axis=-1, keepdims=True)
        var = jnp.mean(jnp.square(x - mu), axis=-1, keepdims=True)
        xn = (x - mu) * jax.lax.rsqrt(var + EPS) * gamma + beta
        logits = jnp.einsum('bsd,de->bse', xn, Wr) + br
        top_vals, top_idx = jax.lax.top_k(logits, K)
        w = jax.nn.softmax(top_vals, axis=-1)
        w_full = jnp.einsum('bsk,bske->bse', w, jax.nn.one_hot(top_idx, E, dtype=w.dtype))
        y = jnp.zeros(x.shape[:-1] + (DOUT,), x.dtype)
        for e in range(E):
            h = jax.nn.gelu(jnp.einsum('bsd,dh->bsh', xn, W1[e]) + b1[e], approximate=False)
            y_e = jnp.einsum('bsh,hd->bsd', h, W2[e]) + b2[e]
            y = y + y_e * w_full[..., e, None]
        return y
    h = _L0_tok_ref(x, L0_tok_W, L0_tok_b)
    h = jnp.concatenate([jnp.broadcast_to(cls_tok, (h.shape[0], 1, h.shape[2])), h], axis=1)
    h = h + _L0_attn_ref(_layernorm(h, axis=-1), L0_attn_Wq, L0_attn_Wk)
    h = h + _L0_ffn_ref(_layernorm(h, axis=-1), L0_ffn_gamma, L0_ffn_beta, L0_ffn_Wr, L0_ffn_br, L0_ffn_W1, L0_ffn_b1, L0_ffn_W2, L0_ffn_b2)
    return h

_drawn_inputs = setup_inputs


def setup_inputs(seed=0):
    import zlib

    import numpy as np

    out = dict(_drawn_inputs(seed))
    spreads = {'L0_ffn_br': (0.0, 0.365)}
    factors = {'cls_tok': 3.915,
     'L0_tok_b': 3.084,
     'L0_ffn_gamma': 8.0,
     'L0_ffn_beta': 8.0,
     'L0_ffn_Wr': 6.459,
     'L0_ffn_W1': 4.409,
     'L0_ffn_b1': 8.0,
     'L0_ffn_W2': 4.367,
     'L0_ffn_b2': 11.761}
    for name, (base, spread) in spreads.items():
        noise = np.random.default_rng([zlib.crc32(name.encode()), seed]).standard_normal(out[name].shape)
        drawn = base * np.exp(spread * noise) if base else spread * noise
        out[name] = jnp.asarray(drawn.astype(out[name].dtype))
    for name, factor in factors.items():
        out[name] = (out[name] * factor).astype(out[name].dtype)
    return out
```

```python
import concourse.bass as bass
from concourse import mybir
from contextlib import ExitStack


def vit_block_program(nc, x, tok_w, columns, wq, wk, w1, b1, wr, br, w2, b2, mats, selectors, priority, out):
    f32 = mybir.dt.float32
    f32r = mybir.dt.float32r
    ALU = mybir.AluOpType
    ACT = mybir.ActivationFunctionType
    AX = mybir.AxisListType

    P = 128
    NQ = x.shape[0]
    KC = x.shape[2]
    PATCHES = x.shape[4] // 2
    N = PATCHES + 1
    T = 2 * N
    D = P // 2
    E = w1.shape[1]
    C = (N + 1) // 2
    START = (0, N - C)
    ROWS = (N - C, C)
    EPS = 1e-5
    CHUNKS = 8
    R = CHUNKS * E
    BANK = 512

    ctx = ExitStack()
    with ctx:
        def sb(name, shape, dt=f32):
            return ctx.enter_context(nc.sbuf_tensor(name, shape, dt))

        def sem(name):
            return ctx.enter_context(nc.semaphore(name))

        tok_w_sb = sb("tok_w_sb", [P, KC, D])
        cols = sb("cols", [P, 4])
        tok_b, cls_tok, gamma, beta = (cols[:, j:j + 1] for j in range(4))
        mats_sb = sb("mats_sb", [P, 3, P])
        center, mean, identity = (mats_sb[:, j, :] for j in range(3))
        wq_sb = sb("wq_sb", [D, D])
        wk_sb = sb("wk_sb", [D, D])
        qk_block = sb("qk_block", [P, P])
        w1_sb = sb("w1_sb", [P, E, P])
        w1_hi = sb("w1_hi", [P, E, P], f32r)
        w1_lo = sb("w1_lo", [P, E, P], f32r)
        b1_sb = sb("b1_sb", [P, E])
        b1_full = sb("b1_full", [P, E])
        wr_sb = sb("wr_sb", [P, E])
        wr_g = sb("wr_g", [P, E])
        wr_hi = sb("wr_hi", [P, E], f32r)
        wr_lo = sb("wr_lo", [P, E], f32r)
        br_sb = sb("br_sb", [P, CHUNKS, E])
        br_full = sb("br_full", [P, CHUNKS, E])
        beta_rows = sb("beta_rows", [D, C])
        w2_sb = sb("w2_sb", [P, E, D])
        b2_sb = sb("b2_sb", [2 * E, D])
        sel_sb = sb("sel_sb", [2 * E, E, P])
        sel_r = sb("sel_r", [2 * E, E, P], f32r)
        prio = sb("prio", [P, CHUNKS, E])
        eps1 = sb("eps1", [P, 1])
        eps2 = sb("eps2", [P, 1])

        h1_store = sb("h1_store", [P, NQ, T])
        xn2_store = sb("xn2_store", [P, NQ, T])

        banks = [ctx.enter_context(nc.psum_tensor(f"bank{b}", [P, BANK], f32)) for b in range(8)]

        weights_loaded = sem("weights_loaded")
        setup_vec = sem("setup_vec")
        setup_mm = sem("setup_mm")

        def wait(engine, semaphore, count):
            if isinstance(count, int) and count <= 0:
                return
            engine.wait_ge(semaphore, count)

        part1 = ExitStack()
        with part1:
            def sb1(name, shape, dt=f32):
                return part1.enter_context(nc.sbuf_tensor(name, shape, dt))

            xt = [sb1(f"xt{p}", [P, KC, 2, 2 * PATCHES]) for p in range(2)]
            h = [sb1(f"hidden{p}", [P, T]) for p in range(2)]
            h1 = sb1("h1_now", [P, T])
            sq1 = sb1("sq1", [P, T])
            sq2 = sb1("sq2", [P, T])
            log1 = sb1("log1", [P, T])
            log2 = sb1("log2", [P, T])
            rstd1 = sb1("rstd1", [P, T])
            rstd2 = sb1("rstd2", [P, T])
            xn = [sb1(f"xn{p}", [P, T]) for p in range(2)]
            z = [sb1(f"z{p}", [P, T]) for p in range(2)]
            xnT = [sb1(f"xnT{p}", [C, 2, 2, P]) for p in range(2)]
            probs = [sb1(f"probs{b}", [C, 2, N]) for b in range(2)]
            probsT = [sb1(f"probsT{b}", [C, 2, N]) for b in range(2)]
            nmax = sb1("nmax", [C, 4, 2])
            psums = sb1("psums", [C, 4, 2])
            rsums = sb1("rsums", [C, 4, 2])

            tok_bank, xc_bank, var_bank = banks[0], banks[1], banks[2]
            s_bank = banks[3:5]
            pT_bank = banks[5:7]
            pv_bank = banks[7]

            x_ready = [sem("x_ready0"), sem("x_ready1")]
            tok_done = sem("tok_done")
            h_ready = sem("h_ready")
            xc1_done, xc2_done = sem("xc1_done"), sem("xc2_done")
            sq1_ready, sq2_ready = sem("sq1_ready"), sem("sq2_ready")
            var1_done, var2_done = sem("var1_done"), sem("var2_done")
            log1_ready, log2_ready = sem("log1_ready"), sem("log2_ready")
            rstd1_ready, rstd2_ready = sem("rstd1_ready"), sem("rstd2_ready")
            xn_ready = sem("xn_ready")
            z_done, z_ready = sem("z_done"), sem("z_ready")
            xnT_done, xnT_ready = sem("xnT_done"), sem("xnT_ready")
            s_done = sem("s_done")
            nmax_ready = sem("nmax_ready")
            exp_done = sem("exp_done")
            rsum_ready = sem("rsum_ready")
            probs_ready = sem("probs_ready")
            pT_done = sem("pT_done")
            pT_ready = [sem("pT_ready0"), sem("pT_ready1")]
            pv_done = sem("pv_done")
            h1_ready = sem("h1_ready")
            h1_kept = sem("h1_kept")
            xn2_ready = sem("xn2_ready")

            def stages(t):
                return [0 <= t + d < NQ for d in (2, 1, 0, -1)]

            ALL = [True] * 4
            PEELED_END = NQ - 2

            def steps(engine, body):
                for t in (-2, -1, 0, 1):
                    body(t, t % 2, stages(t))
                with engine.Fori(1, PEELED_END // 2) as i:
                    for k in range(2):
                        body(2 * i + k, k, ALL)
                for t in range(PEELED_END, NQ + 1):
                    body(t, t % 2, stages(t))

            with nc.Block() as block:
                LOADS = 16

                @block.sync
                def _(sp):
                    for dst, src in ((tok_w_sb[:, :, :], tok_w), (cols[:, :], columns), (mats_sb[:, :, :], mats),
                                     (wq_sb[:, :], wq), (wk_sb[:, :], wk), (w1_sb[:, :, :], w1), (b1_sb[:, :], b1),
                                     (wr_sb[:, :], wr), (br_sb[:, :, :], br), (w2_sb[:, :, :], w2),
                                     (b2_sb[:, :], b2), (sel_sb[:, :, :], selectors), (prio[:, :, :], priority)):
                        sp.dma_start(dst, src).then_inc(weights_loaded, 16)

                    def load(u, p):
                        wait(sp, tok_done, u - 1)
                        sp.dma_start(xt[p][:, :, :, :], x[u, :, :, :, :]).then_inc(x_ready[p], 16)

                    load(0, 0)
                    load(1, 1)
                    with sp.Fori(1, NQ // 2) as i:
                        for k in range(2):
                            load(2 * i + k, k)

                @block.tensor
                def _(pe):
                    pe.wait_ge(weights_loaded, 16 * 13)
                    nc.tensor.matmul(banks[0][0:D, 0:D], wq_sb[:, :], wk_sb[:, :], start=True, stop=True)
                    nc.tensor.matmul(banks[0][D:P, D:P], wq_sb[:, :], wk_sb[:, :], start=True, stop=True)
                    for e in range(E):
                        nc.tensor.matmul(banks[1][:, e:e + 1], w1_sb[0:D, e, :], beta[0:D, :], start=True, stop=True)
                    pe.wait_ge(setup_vec, 2)
                    nc.tensor.matmul(banks[2][0:C, 0:E], beta_rows[:, :], wr_sb[0:D, :], start=True, stop=True)\
                        .then_inc(setup_mm, 1)
                    pe.wait_ge(setup_vec, SETUP_ALL)

                    def embed(c):
                        for half in range(2):
                            last = nc.tensor.matmul(tok_bank[D * half:D * half + D, 0:2 * PATCHES], tok_w_sb[:, c, :],
                                                    xt_now[:, c, half, :], start=(c == 0), stop=(c == KC - 1))
                        return last

                    def body(t, p, has):
                        nonlocal xt_now
                        emb, ln1, att, ln2 = has
                        o = 1 - p
                        xt_now = xt[p]

                        def embedding(third):
                            if third == 0:
                                if isinstance(t, int):
                                    pe.wait_ge(x_ready[p], 16 * ((t + 2) // 2 + 1))
                                else:
                                    pe.wait_ge(x_ready[p], 8 * (t - p) + 32)
                                wait(pe, h_ready, t + 2)
                            for c in range(third * KC // 3, (third + 1) * KC // 3):
                                last = embed(c)
                            if third == 2:
                                last.then_inc(tok_done, 1)

                        def scores(q):
                            k, half = q // 2, q % 2
                            if q == 0:
                                pe.wait_ge(z_ready, t + 1)
                            wait(pe, exp_done, 4 * t + q - 1)
                            a, b = D * half, D * half + D
                            for c in range(2):
                                s = k * N + START[c]
                                last = nc.tensor.matmul(s_bank[half][0:C, c * N:c * N + N], z[p][a:b, s:s + C],
                                                        xn[p][a:b, k * N:k * N + N], start=True, stop=True)
                            last.then_inc(s_done, 1)

                        def transpose_probs(q):
                            half = q % 2
                            pe.wait_ge(probs_ready, 4 * t + q + 1)
                            wait(pe, pT_ready[half], 2 * t + q // 2)
                            for ic in range(2):
                                for jc in range(2):
                                    o0 = jc * N + START[ic]
                                    last = nc.tensor.transpose(pT_bank[half][0:C, o0:o0 + C],
                                                               probs[half][:, ic, START[jc]:START[jc] + C],
                                                               identity[0:C, 0:C])
                            last.then_inc(pT_done, 1)

                        def weigh(q):
                            k, half = q // 2, q % 2
                            pe.wait_ge(pT_ready[half], 2 * t + q // 2 + 1)
                            if q == 0:
                                pe.wait_ge(xnT_ready, t + 1)
                                wait(pe, h1_ready, t)
                            for jc in range(2):
                                last = nc.tensor.matmul(pv_bank[D * half:D * half + D, k * N:k * N + N],
                                                        xnT[p][0:ROWS[jc], k, jc, D * half:D * half + D],
                                                        probsT[half][0:ROWS[jc], jc, :],
                                                        start=(jc == 0), stop=(jc == 1))
                            last.then_inc(pv_done, 1)

                        if att:
                            scores(0)
                            scores(1)
                        if ln1:
                            pe.wait_ge(h_ready, t + 2)
                            wait(pe, xn2_ready, t - 1)
                            nc.tensor.matmul(xc_bank[:, 0:T], center, h[o][:, :], start=True, stop=True)\
                                .then_inc(xc1_done, 1)
                        if emb:
                            embedding(0)
                        if ln1:
                            pe.wait_ge(sq1_ready, t + 2)
                            wait(pe, log2_ready, t - 1)
                            nc.tensor.matmul(var_bank[:, 0:T], mean, sq1[:, :], start=True, stop=True)\
                                .then_inc(var1_done, 1)
                        if att:
                            transpose_probs(0)
                            scores(2)
                            transpose_probs(1)
                        if emb:
                            embedding(1)
                        if ln1:
                            pe.wait_ge(xn_ready, t + 2)
                            nc.tensor.matmul(var_bank[:, 0:T], qk_block[:, :], xn[o][:, :], start=True, stop=True)\
                                .then_inc(z_done, 1)
                        if att:
                            weigh(0)
                            scores(3)
                        if ln1:
                            wait(pe, pT_ready[1], 2 * t + 1)
                            for k in range(2):
                                for jc in range(2):
                                    s = k * N + START[jc]
                                    c0 = (2 * k + jc) * P
                                    last = nc.tensor.transpose(pT_bank[1][0:C, c0:c0 + P], xn[o][:, s:s + C], identity)
                            last.then_inc(xnT_done, 1)
                        if att:
                            weigh(1)
                        if ln2:
                            if ln1:
                                pass
                            pe.wait_ge(h1_ready, t)
                            wait(pe, xn_ready, min(t + 2, NQ) if isinstance(t, int) else t + 2)
                            if isinstance(t, int):
                                wait(pe, xn2_ready, t - 1)
                            nc.tensor.matmul(xc_bank[:, 0:T], center, h1[:, :], start=True, stop=True)\
                                .then_inc(xc2_done, 1)
                        if att:
                            transpose_probs(2)
                        if emb:
                            embedding(2)
                        if ln2:
                            pe.wait_ge(sq2_ready, t)
                            pe.wait_ge(z_ready, min(t + 2, NQ) if isinstance(t, int) else t + 2)
                            if isinstance(t, int):
                                wait(pe, log2_ready, t - 1)
                            nc.tensor.matmul(var_bank[:, 0:T], mean, sq2[:, :], start=True, stop=True)\
                                .then_inc(var2_done, 1)
                        if att:
                            if ln1:
                                pe.wait_ge(xnT_ready, t + 2)
                            transpose_probs(3)
                            weigh(2)
                            weigh(3)

                    xt_now = None
                    steps(pe, body)

                @block.scalar
                def _(act):
                    act.preload_act_table_set("natural_log_exp_and_others")
                    act.wait_ge(setup_vec, SETUP_ALL)

                    def body(t, p, has):
                        emb, ln1, att, ln2 = has
                        o = 1 - p

                        def exps(q):
                            half = q % 2
                            act.wait_ge(nmax_ready, 4 * t + q + 1)
                            wait(act, pT_done, 4 * t + q - 1)
                            for c in range(2):
                                last = nc.scalar.activation(probs[half][:, c, :], s_bank[half][0:C, c * N:c * N + N],
                                                            ACT.Exp, bias=nmax[:, q, c:c + 1],
                                                            accum_out=psums[:, q, c:c + 1])
                            last.then_inc(exp_done, 1)

                        def take_probsT(q):
                            act.wait_ge(pT_done, 4 * t + q + 1)
                            wait(act, pv_done, 4 * t + q - 1)
                            nc.scalar.copy(probsT[0][:, :, :], pT_bank[0][0:C, 0:T].rearrange("p (c n) -> p c n", c=2))\
                                .then_inc(pT_ready[0], 1)

                        if att:
                            exps(0)
                        if ln1:
                            act.wait_ge(xc1_done, t + 2)
                            wait(act, var1_done, t + 1)
                            nc.scalar.activation(sq1[:, :], xc_bank[:, 0:T], ACT.Square).then_inc(sq1_ready, 1)
                        if att:
                            exps(1)
                        if ln1:
                            act.wait_ge(var1_done, t + 2)
                            nc.scalar.activation(log1[:, :], var_bank[:, 0:T], ACT.Ln, bias=eps1[:, :])\
                                .then_inc(log1_ready, 1)
                            act.wait_ge(log1_ready, t + 2)
                            wait(act, xn_ready, t + 1)
                            nc.scalar.activation(rstd1[:, :], log1[:, :], ACT.Exp, scale=-0.5)\
                                .then_inc(rstd1_ready, 1)
                        if att:
                            take_probsT(0)
                            exps(2)
                            exps(3)
                        if ln2:
                            act.wait_ge(xc2_done, t)
                            wait(act, var2_done, t - 1)
                            nc.scalar.activation(sq2[:, :], xc_bank[:, 0:T], ACT.Square).then_inc(sq2_ready, 1)
                        if att:
                            take_probsT(2)
                        if ln2:
                            act.wait_ge(var2_done, t)
                            nc.scalar.activation(log2[:, :], var_bank[:, 0:T], ACT.Ln, bias=eps2[:, :], scale=1.0 + EPS)\
                                .then_inc(log2_ready, 1)
                            act.wait_ge(log2_ready, t)
                            wait(act, xn2_ready, t - 1)
                            nc.scalar.activation(rstd2[:, :], log2[:, :], ACT.Exp, scale=-0.5)\
                                .then_inc(rstd2_ready, 1)
                        if emb:
                            act.wait_ge(tok_done, t + 3)
                            wait(act, h1_ready, t + 1)
                            nc.scalar.activation(h[p][:, :].rearrange("p (k n) -> p k n", k=2)[:, :, 1:N],
                                                 tok_bank[:, 0:2 * PATCHES].rearrange("p (k n) -> p k n", k=2),
                                                 ACT.Identity, bias=tok_b).then_inc(h_ready, 1)

                    steps(act, body)

                @block.vector
                def _(dve):
                    count = [0]

                    def done(instruction):
                        count[0] += 1
                        instruction.then_inc(setup_vec, 1)
                        dve.wait_ge(setup_vec, count[0])

                    dve.wait_ge(weights_loaded, 16 * 13)
                    done(nc.vector.memset(eps1[:, :], EPS))
                    done(nc.vector.tensor_copy(beta_rows[:, :], beta[0:D, :].to_broadcast([D, C])))
                    done(nc.vector.memset(eps2[:, :], EPS * EPS))
                    done(nc.vector.memset(qk_block[:, :], 0.0))
                    for p in range(2):
                        done(nc.vector.tensor_copy(h[p][:, :].rearrange("p (k n) -> p k n", k=2)[:, :, 0],
                                                   cls_tok.to_broadcast([P, 2])))
                    dve.wait_ge(setup_mm, 1)
                    nc.vector.tensor_tensor(b1_full[:, :], banks[1][:, 0:E], b1_sb[:, :], ALU.add)
                    nc.vector.tensor_tensor(br_full[0:C, :, :], br_sb[0:C, :, :],
                                            banks[2][0:C, 0:E].unsqueeze(1).to_broadcast([C, CHUNKS, E]), ALU.add)
                    for half in range(2):
                        a, b = D * half, D * half + D
                        nc.vector.tensor_scalar(qk_block[a:b, a:b], banks[0][a:b, a:b], float(D) ** -0.5, None, ALU.mult)
                    nc.vector.tensor_scalar(wr_g[:, :], wr_sb[:, :], gamma, None, ALU.mult)
                    nc.vector.tensor_copy(sel_r[:, :, :], sel_sb[:, :, :])
                    done(nc.vector.tensor_scalar(w1_sb[:, :, :], w1_sb[:, :, :], gamma, None, ALU.mult))
                    nc.vector.tensor_copy(wr_hi[:, :], wr_g[:, :])
                    done(nc.vector.tensor_copy(w1_hi[:, :, :], w1_sb[:, :, :]))
                    nc.vector.tensor_tensor(wr_lo[:, :], wr_g[:, :], wr_hi[:, :].bitcast(f32), ALU.subtract)
                    done(nc.vector.tensor_tensor(w1_lo[:, :, :], w1_sb[:, :, :], w1_hi[:, :, :].bitcast(f32), ALU.subtract))
                    assert count[0] == SETUP_ALL

                    def body(t, p, has):
                        emb, ln1, att, ln2 = has
                        o = 1 - p

                        def maxima(q):
                            half = q % 2
                            dve.wait_ge(s_done, 4 * t + q + 1)
                            nc.vector.tensor_reduce(nmax[:, q, :], s_bank[half][0:C, 0:T].rearrange("p (c n) -> p c n", c=2),
                                                    axis=AX.X, op=ALU.max, negate=True).then_inc(nmax_ready, 1)

                        def reciprocals(q):
                            dve.wait_ge(exp_done, 4 * t + q + 1)
                            nc.vector.reciprocal(rsums[:, q, :], psums[:, q, :]).then_inc(rsum_ready, 1)

                        def take_probsT(q):
                            dve.wait_ge(pT_done, 4 * t + q + 1)
                            wait(dve, pv_done, 4 * t + q - 1)
                            nc.vector.tensor_copy(probsT[1][:, :, :],
                                                  pT_bank[1][0:C, 0:T].rearrange("p (c n) -> p c n", c=2))\
                                .then_inc(pT_ready[1], 1)

                        if att:
                            maxima(0)
                            reciprocals(0)
                            maxima(1)
                            reciprocals(1)
                        if ln1:
                            dve.wait_ge(rstd1_ready, t + 2)
                            nc.vector.tensor_tensor(xn[o][:, :], xc_bank[:, 0:T], rstd1[:, :], ALU.mult)\
                                .then_inc(xn_ready, 1)
                        if att:
                            maxima(2)
                            take_probsT(1)
                            reciprocals(2)
                        if ln1:
                            dve.wait_ge(z_done, t + 2)
                            nc.vector.tensor_copy(z[o][:, :], var_bank[:, 0:T]).then_inc(z_ready, 1)
                        if att:
                            maxima(3)
                        if ln1:
                            dve.wait_ge(xnT_done, t + 2)
                            nc.vector.tensor_copy(xnT[o][:, :, :, :],
                                                  pT_bank[1][0:C, :].rearrange("p (k j d) -> p k j d", k=2, j=2))\
                                .then_inc(xnT_ready, 1)
                        if att:
                            reciprocals(3)
                            take_probsT(3)
                            dve.wait_ge(pv_done, 4 * t + 4)
                            wait(dve, xc2_done, t)
                            wait(dve, h1_kept, t)
                            nc.vector.tensor_tensor(h1[:, :], pv_bank[:, 0:T], h[p][:, :], ALU.add)\
                                .then_inc(h1_ready, 1)
                        if ln2:
                            dve.wait_ge(rstd2_ready, t)
                            nc.vector.tensor_tensor(xn2_store[:, t - 1, :], xc_bank[:, 0:T], rstd2[:, :], ALU.mult)\
                                .then_inc(xn2_ready, 1)

                    steps(dve, body)

                @block.gpsimd
                def _(pool):
                    def body(t, p, has):
                        emb, ln1, att, ln2 = has
                        if ln2:
                            pool.wait_ge(h1_ready, t)
                            nc.gpsimd.tensor_copy(h1_store[:, t - 1, :], h1[:, :]).then_inc(h1_kept, 1)
                        if att:
                            for q in range(4):
                                half = q % 2
                                pool.wait_ge(rsum_ready, 4 * t + q + 1)
                                nc.gpsimd.tensor_tensor(probs[half][:, :, :], probs[half][:, :, :],
                                                        rsums[:, q, :].unsqueeze(2).to_broadcast([C, 2, N]), ALU.mult)\
                                    .then_inc(probs_ready, 1)

                    steps(pool, body)

        part2 = ExitStack()
        with part2:
            def sb2(name, shape, dt=f32):
                return part2.enter_context(nc.sbuf_tensor(name, shape, dt))

            x2 = [[sb2(f"x2_{p}{half}", [P, T], f32r) for half in range(2)] for p in range(2)]
            gelu = [[sb2(f"gelu{b}{half}", [P, T]) for half in range(2)] for b in range(2)]
            scaled = [[sb2(f"scaled{b}{half}", [P, T]) for half in range(2)] for b in range(2)]
            wT = [[sb2(f"wT{p}{half}", [2 * E, T], f32r) for half in range(2)] for p in range(2)]
            result = [sb2(f"result{p}", [P, T]) for p in range(2)]
            logits = sb2("logits", [C, CHUNKS, E])
            rest = sb2("rest", [C, CHUNKS, E])
            is_max = sb2("is_max", [C, CHUNKS, E])
            ranked = sb2("ranked", [C, CHUNKS, E])
            first = sb2("first", [C, CHUNKS, E])
            second = sb2("second", [C, CHUNKS, E])
            top1 = sb2("top1", [C, CHUNKS])
            top2 = sb2("top2", [C, CHUNKS])
            best = sb2("best", [C, CHUNKS])
            gap = sb2("gap", [C, CHUNKS])
            tanh_gap = sb2("tanh_gap", [C, CHUNKS])
            weight1 = sb2("weight1", [C, CHUNKS])
            weight2 = sb2("weight2", [C, CHUNKS])
            part_a = sb2("part_a", [C, CHUNKS, E])
            part_b = sb2("part_b", [C, CHUNKS, E])
            weights = sb2("weights", [C, CHUNKS, E])
            w_split = sb2("w_split", [C, CHUNKS, 2, E])

            z1_bank = banks[0:2]
            wb_bank = banks[2:4]
            y_bank = banks[4:6]
            r_bank = banks[6:8]

            x2_hi_ready, x2_lo_ready = sem("x2_hi_ready"), sem("x2_lo_ready")
            logits_done = sem("logits_done")
            router_vec = sem("router_vec")
            tanh_ready = sem("tanh_ready")
            router_pool = sem("router_pool")
            wT_done, wT_ready = sem("wT_done"), sem("wT_ready")
            z1_done = sem("z1_done")
            gelu_ready = sem("gelu_ready")
            wb_done = sem("wb_done")
            scaled_ready = sem("scaled_ready")
            y_done = sem("y_done")
            result_ready = sem("result_ready")
            out_stored = [sem("out_stored0"), sem("out_stored1")]

            VEC = 15
            POOL = 5

            def quads(engine, body):
                body(0, 0, True, True)
                body(1, 1, True, True)
                with engine.Fori(1, NQ // 2 - 1) as i:
                    for k in range(2):
                        body(2 * i + k, k, True, True)
                body(NQ - 2, 0, True, False)
                body(NQ - 1, 1, False, False)

            with nc.Block() as block:

                @block.tensor
                def _(pe):
                    def first_layer(u, p, e):
                        if e == 0:
                            pe.wait_ge(x2_hi_ready, 2 * u + 2)
                            pe.wait_ge(x2_lo_ready, 2 * u + 2)
                        for half in range(2):
                            wait(pe, gelu_ready, 16 * u + 2 * e + half - 1)
                            nc.tensor.matmul(z1_bank[half][:, 0:T], w1_hi[:, e, :], x2[p][half][:, :], start=True, stop=False)
                            nc.tensor.matmul(z1_bank[half][:, 0:T], w1_lo[:, e, :], x2[p][half][:, :], start=False, stop=True)\
                                .then_inc(z1_done, 1)

                    def spread_weights(u, p, e):
                        if e == 0:
                            pe.wait_ge(wT_ready, 2 * u + 2)
                        for half in range(2):
                            wait(pe, scaled_ready, 16 * u + 2 * e + half - 1)
                            nc.tensor.matmul(wb_bank[half][:, 0:T], sel_r[:, e, :], wT[p][half][:, :], start=True, stop=True)\
                                .then_inc(wb_done, 1)

                    def second_layer(u, p, e):
                        if e == 0:
                            wait(pe, result_ready, u - 1)
                            for half in range(2):
                                nc.tensor.matmul(y_bank[p][D * half:D * half + D, 0:T], b2_sb[:, :],
                                                 wT[p][half][:, :].bitcast(f32), start=True, stop=False)
                        pe.wait_ge(scaled_ready, 16 * u + 2 * e + 2)
                        for half in range(2):
                            last = nc.tensor.matmul(y_bank[p][D * half:D * half + D, 0:T], w2_sb[:, e, :],
                                                    scaled[e % 2][half][:, :], start=False, stop=(e == E - 1))
                        if e == E - 1:
                            last.then_inc(y_done, 1)

                    def route(u, p):
                        pe.wait_ge(x2_hi_ready, 2 * u + 2)
                        pe.wait_ge(x2_lo_ready, 2 * u + 2)
                        wait(pe, wT_ready, 2 * u)
                        for n in range(CHUNKS):
                            half, s = n // 4, (n // 2 % 2) * N + START[n % 2]
                            nc.tensor.matmul(r_bank[0][0:C, n * E:n * E + E], x2[p][half][:, s:s + C], wr_hi[:, :],
                                             start=True, stop=False)
                            last = nc.tensor.matmul(r_bank[0][0:C, n * E:n * E + E], x2[p][half][:, s:s + C], wr_lo[:, :],
                                                    start=False, stop=True)
                        last.then_inc(logits_done, 1)

                    def transpose_weights(u):
                        pe.wait_ge(router_pool, POOL * u + POOL)
                        for n in range(CHUNKS):
                            half, s = n // 4, (n // 2 % 2) * N + START[n % 2]
                            last = nc.tensor.transpose(r_bank[half][0:2 * E, s:s + C],
                                                       w_split[:, n, :, :].rearrange("p a e -> p (a e)"), identity[0:C, 0:C])
                            if n % 4 == 3:
                                last.then_inc(wT_done, 1)

                    def body(u, p, has_next, _):
                        for e in range(E):
                            last_step = e == E - 1
                            if not last_step:
                                first_layer(u, p, e + 1)
                            elif has_next:
                                first_layer(u + 1, 1 - p, 0)
                            if e == 6 and has_next:
                                transpose_weights(u + 1)
                            if not last_step:
                                spread_weights(u, p, e + 1)
                            elif has_next:
                                spread_weights(u + 1, 1 - p, 0)
                            second_layer(u, p, e)
                            if e == 0 and has_next:
                                route(u + 1, 1 - p)

                    route(0, 0)
                    first_layer(0, 0, 0)
                    transpose_weights(0)
                    spread_weights(0, 0, 0)
                    quads(pe, body)

                @block.scalar
                def _(act):
                    act.preload_act_table_set("gelu_and_others")

                    def split_hi(u, p):
                        wait(act, z1_done, 16 * u - 16)
                        for half in range(2):
                            a, b = D * half, D * half + D
                            nc.scalar.copy(x2[p][half][a:b, :], xn2_store[a:b, u, :]).then_inc(x2_hi_ready, 1)

                    def tanh(u):
                        act.wait_ge(router_vec, VEC * u + 13)
                        nc.scalar.activation(tanh_gap[:, :], gap[:, :], ACT.Tanh, scale=0.5).then_inc(tanh_ready, 1)

                    def take_wT(u, p):
                        for half in range(2):
                            act.wait_ge(wT_done, 2 * u + half + 1)
                            wait(act, y_done, u - 1)
                            nc.scalar.copy(wT[p][half][:, :], r_bank[half][0:2 * E, 0:T]).then_inc(wT_ready, 1)

                    def body(u, p, has_next, has_after_next):
                        for e in range(E):
                            for half in range(2):
                                n = 16 * u + 2 * e + half
                                act.wait_ge(z1_done, n + 1)
                                wait(act, scaled_ready, n - 3)
                                nc.scalar.activation(gelu[e % 2][half][:, :], z1_bank[half][:, 0:T], ACT.Gelu,
                                                     bias=b1_full[:, e:e + 1]).then_inc(gelu_ready, 1)
                            if e == 5 and has_next:
                                tanh(u + 1)
                        if has_next:
                            take_wT(u + 1, 1 - p)
                        if has_after_next:
                            split_hi(u + 2, p)

                    split_hi(0, 0)
                    tanh(0)
                    take_wT(0, 0)
                    split_hi(1, 1)
                    quads(act, body)

                @block.vector
                def _(dve):
                    def top_two(u, r):
                        b = VEC * u
                        wide = [C, CHUNKS, E]
                        if r == 0:
                            dve.wait_ge(logits_done, u + 1)
                        else:
                            dve.wait_ge(router_vec, b + r)
                        if r == 0:
                            step = nc.vector.tensor_tensor(logits[:, :, :], r_bank[0][0:C, 0:R].rearrange("p (c e) -> p c e", e=E),
                                                           br_full[0:C, :, :], ALU.add)
                        elif r == 1:
                            step = nc.vector.tensor_reduce(top1[:, :], logits[:, :, :], axis=AX.X, op=ALU.max)
                        elif r == 2:
                            step = nc.vector.tensor_tensor(is_max[:, :, :], logits[:, :, :],
                                                           top1[:, :].unsqueeze(2).to_broadcast(wide), ALU.is_equal)
                        elif r == 3:
                            step = nc.vector.tensor_tensor(ranked[:, :, :], is_max[:, :, :], prio[0:C, :, :], ALU.mult)
                        elif r == 4:
                            step = nc.vector.tensor_reduce(best[:, :], ranked[:, :, :], axis=AX.X, op=ALU.max)
                        elif r == 5:
                            wait(dve, router_pool, POOL * u)
                            step = nc.vector.tensor_tensor(first[:, :, :], ranked[:, :, :],
                                                           best[:, :].unsqueeze(2).to_broadcast(wide), ALU.is_equal)
                        elif r == 6:
                            step = nc.vector.scalar_tensor_tensor(rest[:, :, :], first[:, :, :], -3.0e38, logits[:, :, :],
                                                                  ALU.mult, ALU.add)
                        elif r == 7:
                            step = nc.vector.tensor_reduce(top2[:, :], rest[:, :, :], axis=AX.X, op=ALU.max)
                        elif r == 8:
                            step = nc.vector.tensor_tensor(is_max[:, :, :], rest[:, :, :],
                                                           top2[:, :].unsqueeze(2).to_broadcast(wide), ALU.is_equal)
                        elif r == 9:
                            step = nc.vector.tensor_tensor(ranked[:, :, :], is_max[:, :, :], prio[0:C, :, :], ALU.mult)
                        elif r == 10:
                            step = nc.vector.tensor_reduce(best[:, :], ranked[:, :, :], axis=AX.X, op=ALU.max)
                        elif r == 11:
                            step = nc.vector.tensor_tensor(second[:, :, :], ranked[:, :, :],
                                                           best[:, :].unsqueeze(2).to_broadcast(wide), ALU.is_equal)
                        elif r == 12:
                            step = nc.vector.tensor_tensor(gap[:, :], top1[:, :], top2[:, :], ALU.subtract)
                        step.then_inc(router_vec, 1)

                    def pair_weights(u):
                        dve.wait_ge(tanh_ready, u + 1)
                        nc.vector.tensor_scalar(weight1[:, :], tanh_gap[:, :], 0.5, 0.5, ALU.mult, ALU.add)\
                            .then_inc(router_vec, 1)
                        nc.vector.tensor_scalar(weight2[:, :], tanh_gap[:, :], -0.5, 0.5, ALU.mult, ALU.add)\
                            .then_inc(router_vec, 1)

                    def body(u, p, has_next, _):
                        for e in range(E):
                            for half in range(2):
                                n = 16 * u + 2 * e + half
                                dve.wait_ge(gelu_ready, n + 1)
                                dve.wait_ge(wb_done, n + 1)
                                nc.vector.tensor_tensor(scaled[e % 2][half][:, :], wb_bank[half][:, 0:T],
                                                        gelu[e % 2][half][:, :], ALU.mult).then_inc(scaled_ready, 1)
                            if has_next:
                                for r in {2: range(0, 5), 3: range(5, 9), 4: range(9, 13)}.get(e, ()):
                                    top_two(u + 1, r)
                                if e == 5:
                                    pair_weights(u + 1)
                        dve.wait_ge(y_done, u + 1)
                        if isinstance(u, int):
                            wait(dve, out_stored[p], 16 * (u // 2))
                        else:
                            dve.wait_ge(out_stored[p], 8 * (u - p))
                        nc.vector.tensor_tensor(result[p][:, :], y_bank[p][:, 0:T], h1_store[:, u, :], ALU.add)\
                            .then_inc(result_ready, 1)

                    for r in range(13):
                        top_two(0, r)
                    pair_weights(0)
                    quads(dve, body)

                @block.gpsimd
                def _(pool):
                    def split_lo(u, p):
                        for half in range(2):
                            a, b = D * half, D * half + D
                            c, d = D * (1 - half), D * (1 - half) + D
                            pool.wait_ge(x2_hi_ready, 2 * u + half + 1)
                            nc.gpsimd.tensor_tensor(x2[p][half][c:d, :], xn2_store[a:b, u, :],
                                                    x2[p][half][a:b, :].bitcast(f32), ALU.subtract)\
                                .then_inc(x2_lo_ready, 1)

                    def token_weights(u):
                        b = POOL * u
                        wide = [C, CHUNKS, E]
                        pool.wait_ge(router_vec, VEC * u + VEC)
                        nc.gpsimd.tensor_tensor(part_a[:, :, :], first[:, :, :],
                                                weight1[:, :].unsqueeze(2).to_broadcast(wide), ALU.mult).then_inc(router_pool, 1)
                        nc.gpsimd.tensor_tensor(part_b[:, :, :], second[:, :, :],
                                                weight2[:, :].unsqueeze(2).to_broadcast(wide), ALU.mult).then_inc(router_pool, 1)
                        pool.wait_ge(router_pool, b + 2)
                        wait(pool, wT_done, 2 * u)
                        nc.gpsimd.tensor_tensor(weights[:, :, :], part_a[:, :, :], part_b[:, :, :], ALU.add).then_inc(router_pool, 1)
                        nc.gpsimd.tensor_tensor(w_split[:, :, 0, :].bitcast(f32r), part_a[:, :, :], part_b[:, :, :], ALU.add)\
                            .then_inc(router_pool, 1)
                        pool.wait_ge(router_pool, b + 4)
                        nc.gpsimd.tensor_tensor(w_split[:, :, 1, :], weights[:, :, :], w_split[:, :, 0, :], ALU.subtract)\
                            .then_inc(router_pool, 1)

                    def body(u, p, has_next, has_after_next):
                        if has_next:
                            token_weights(u + 1)
                        if has_after_next:
                            split_lo(u + 2, p)

                    split_lo(0, 0)
                    token_weights(0)
                    split_lo(1, 1)
                    quads(pool, body)

                @block.sync
                def _(sp):
                    def body(u, p, *_):
                        sp.wait_ge(result_ready, u + 1)
                        sp.dma_start(out[u, :, :], result[p][:, :]).then_inc(out_stored[p], 16)

                    quads(sp, body)
                    for p in range(2):
                        sp.wait_ge(out_stored[p], 16 * (NQ // 2))


SETUP_ALL = 9


def kernel(**inputs):
    import numpy as np
    import concourse.bacc as bacc
    from concourse import mybir
    from concourse.bass_utils import run_bass_kernel_spmd

    a = {k: np.asarray(v) for k, v in inputs.items()}
    PATCH, PARTS = 16, 128
    B, CH, H, W = a["x"].shape
    nh, nw = H // PATCH, W // PATCH
    D = a["L0_tok_W"].shape[0]
    E = a["L0_ffn_W1"].shape[0]
    NQ = B // 4
    rows = PARTS // PATCH
    chunks = PATCH // rows

    x = a["x"].reshape(NQ, 2, 2, CH, nh, chunks, rows, nw, PATCH).transpose(0, 6, 8, 3, 5, 1, 2, 4, 7)
    x = np.ascontiguousarray(x).reshape(NQ, PARTS, CH * chunks, 2, 2 * nh * nw)
    twice = lambda m: np.concatenate([m, m], axis=0)
    arrays = {
        "x": x,
        "tok_w": a["L0_tok_W"].T.reshape(CH * chunks, PARTS, D).transpose(1, 0, 2),
        "columns": twice(np.stack([a["L0_tok_b"], a["cls_tok"].reshape(D), a["L0_ffn_gamma"], a["L0_ffn_beta"]], axis=1)),
        "wq": a["L0_attn_Wq"],
        "wk": a["L0_attn_Wk"],
        "w1": twice(a["L0_ffn_W1"].transpose(1, 0, 2)),
        "b1": a["L0_ffn_b1"].T,
        "wr": twice(a["L0_ffn_Wr"]),
        "br": np.broadcast_to(a["L0_ffn_br"], (PARTS, 8, E)),
        "w2": a["L0_ffn_W2"].transpose(1, 0, 2),
        "b2": twice(a["L0_ffn_b2"]),
    }
    blocks = np.kron(np.eye(2), np.ones((D, D))) / D
    arrays["mats"] = np.stack([np.eye(PARTS) - blocks, blocks, np.eye(PARTS)], axis=1)
    arrays["selectors"] = np.broadcast_to(np.tile(np.eye(E), (2, 1))[:, :, None], (2 * E, E, PARTS))
    arrays["priority"] = np.broadcast_to(np.arange(E, 0, -1), (PARTS, 8, E))

    nc = bacc.Bacc("TRN2", target_bir_lowering=False, num_devices=1)
    feeds, handles = {}, {}
    for name, value in arrays.items():
        feeds[name + "_in"] = np.ascontiguousarray(value, dtype=np.float32)
        handles[name] = nc.dram_tensor(name + "_in", value.shape, mybir.dt.float32, kind="ExternalInput").ap()
    N = nh * nw + 1
    out = nc.dram_tensor("tokens_out", (NQ, PARTS, 2 * N), mybir.dt.float32, kind="ExternalOutput").ap()
    vit_block_program(nc, out=out, **handles)
    got = run_bass_kernel_spmd(nc, [feeds], core_ids=[0]).results[0]["tokens_out"]
    return got.reshape(NQ, 2, D, 2, N).transpose(0, 1, 3, 4, 2).reshape(B, N, D)
```

```python
import concourse.bass as bass
from concourse import mybir
from contextlib import ExitStack


def vit_block_program(nc, x, tok_w, columns, wq, wk, w1, b1, wr, br, w2, b2, mats, selectors, priority, out):
    f32 = mybir.dt.float32
    f32r = mybir.dt.float32r
    ALU = mybir.AluOpType
    ACT = mybir.ActivationFunctionType
    AX = mybir.AxisListType

    P = 128
    NQ = x.shape[0]
    KC = x.shape[2]
    PATCHES = x.shape[4] // 2
    N = PATCHES + 1
    T = 2 * N
    D = P // 2
    E = w1.shape[1]
    C = (N + 1) // 2
    START = (0, N - C)
    ROWS = (N - C, C)
    EPS = 1e-5
    CHUNKS = 4
    S = 4 * E
    BANK = 512

    ctx = ExitStack()
    with ctx:
        def sb(name, shape, dt=f32):
            return ctx.enter_context(nc.sbuf_tensor(name, shape, dt))

        def sem(name):
            return ctx.enter_context(nc.semaphore(name))

        tok_w_sb = sb("tok_w_sb", [P, KC, D])
        cols = sb("cols", [P, 4])
        tok_b, cls_tok, gamma, beta = (cols[:, j:j + 1] for j in range(4))
        mats_sb = sb("mats_sb", [P, 3, P])
        center, mean, identity = (mats_sb[:, j, :] for j in range(3))
        wq_sb = sb("wq_sb", [D, D])
        wk_sb = sb("wk_sb", [D, D])
        qk_block = sb("qk_block", [P, P])
        w1_hi = sb("w1_hi", [P, E, P], f32r)
        w1_lo = sb("w1_lo", [P, E, P], f32r)
        b1_sb = sb("b1_sb", [P, E])
        b1_full = sb("b1_full", [P, E])
        wr_sb = sb("wr_sb", [P, E])
        wr_block = sb("wr_block", [P, P])
        br_sb = sb("br_sb", [P, CHUNKS, 2, E])
        br_full = sb("br_full", [P, CHUNKS, 2, E])
        beta_rows = sb("beta_rows", [D, C])
        w2_sb = sb("w2_sb", [P, E, D])
        b2_sb = sb("b2_sb", [S, P])
        b2_hi = sb("b2_hi", [S, P], f32r)
        b2_lo = sb("b2_lo", [S, P], f32r)
        sel_r = sb("sel_r", [S, 2, E, P], f32r)
        prio = sb("prio", [P, CHUNKS, 2, E])
        eps1 = sb("eps1", [P, 1])
        eps2 = sb("eps2", [P, 1])

        h1_store = sb("h1_store", [P, NQ, T])
        xn2_store = sb("xn2_store", [P, NQ, T])
        staging = h1_store[:, :, :].rearrange("p q t -> p (q t)")
        w1_sb = staging[:, 0:E * P].rearrange("p (e h) -> p e h", e=E)
        sel_sb = staging[0:S, E * P:3 * E * P].rearrange("p (a e h) -> p a e h", a=2, e=E)
        w_store = sb("w_store", [C, NQ, CHUNKS, 2, E])

        banks = [ctx.enter_context(nc.psum_tensor(f"bank{b}", [P, BANK], f32)) for b in range(8)]

        weights_loaded = sem("weights_loaded")
        setup_vec = sem("setup_vec")
        setup_mm = sem("setup_mm")

        def wait(engine, semaphore, count):
            if isinstance(count, int) and count <= 0:
                return
            engine.wait_ge(semaphore, count)

        part1 = ExitStack()
        with part1:
            def sb1(name, shape, dt=f32):
                return part1.enter_context(nc.sbuf_tensor(name, shape, dt))

            xt = [sb1(f"xt{p}", [P, KC, 2, 2 * PATCHES]) for p in range(2)]
            h = [sb1(f"hidden{p}", [P, T]) for p in range(2)]
            xc1 = [sb1(f"xc1_{p}", [P, T]) for p in range(2)]
            xc2 = sb1("xc2", [P, T])
            xn2 = sb1("xn2", [P, T])
            stat1 = sb1("stat1", [P, T])
            stat2 = sb1("stat2", [P, T])
            xn = [sb1(f"xn{p}", [P, T]) for p in range(2)]
            z = [sb1(f"z{p}", [P, T]) for p in range(2)]
            xnT = [sb1(f"xnT{p}", [C, 2, 2, P]) for p in range(2)]
            probs = [sb1(f"probs{b}", [C, 2, N]) for b in range(2)]
            probsT = [sb1(f"probsT{b}", [C, 2, N]) for b in range(2)]
            nmax = sb1("nmax", [C, 4, 2])
            psums = sb1("psums", [C, 4, 2])
            rsums = sb1("rsums", [C, 4, 2])
            WIDE = [C, CHUNKS, 2, E]
            logitsT = sb1("logitsT", [P, T])
            logits = sb1("logits", WIDE)
            rest = sb1("rest", WIDE)
            is_max = sb1("is_max", WIDE)
            ranked = sb1("ranked", WIDE)
            first = sb1("first", WIDE)
            second = sb1("second", WIDE)
            part_a = sb1("part_a", WIDE)
            part_b = sb1("part_b", WIDE)
            top1, top2, best, gap, exp_gap, sum_exp, weight1, weight2 = (
                sb1(name, [C, CHUNKS, 2]) for name in
                ("top1", "top2", "best", "gap", "exp_gap", "sum_exp", "weight1", "weight2"))

            tok_bank = banks[0]
            xc_bank = banks[1]
            var_bank = banks[2]
            s_bank = banks[3:5]
            pT_bank = banks[5:7]
            pv_bank = banks[7]

            x_ready = [sem("x_ready0"), sem("x_ready1")]
            tok_done = sem("tok_done")
            h_ready = sem("h_ready")
            h_kept = sem("h_kept")
            xc1_done = sem("xc1_done")
            xc1_ready, xc2_ready = sem("xc1_ready"), sem("xc2_ready")
            sq1_ready, sq2_ready = sem("sq1_ready"), sem("sq2_ready")
            var1_done, var2_done = sem("var1_done"), sem("var2_done")
            log1_ready, log2_ready = sem("log1_ready"), sem("log2_ready")
            rstd1_ready, rstd2_ready = sem("rstd1_ready"), sem("rstd2_ready")
            xn_ready = sem("xn_ready")
            z_done, z_ready = sem("z_done"), sem("z_ready")
            xnT_done, xnT_ready = sem("xnT_done"), sem("xnT_ready")
            s_done = sem("s_done")
            nmax_ready = sem("nmax_ready")
            exp_done = sem("exp_done")
            rsum_ready = sem("rsum_ready")
            probs_ready = sem("probs_ready")
            pT_done = sem("pT_done")
            pT_ready = [sem("pT_ready0"), sem("pT_ready1")]
            pv_done = sem("pv_done")
            h1_ready = sem("h1_ready")
            xn2_ready = sem("xn2_ready")
            xn2_kept = sem("xn2_kept")
            logitsT_done, logitsT_ready = sem("logitsT_done"), sem("logitsT_ready")
            logits_done = sem("logits_done")
            logits_ready = sem("logits_ready")
            router_vec = sem("router_vec")
            exp_gap_ready = sem("exp_gap_ready")
            router_pool = sem("router_pool")
            VEC = 15
            POOL = 3

            def stages(t):
                return [0 <= t + d < NQ for d in (2, 1, 0, -1, -2)]

            ALL = [True] * 5
            PEELED_END = NQ - 2
            EMBED = (range(0, 2), range(2, 4), range(4, 5), range(5, KC))

            def last_quad(count):
                return min(count, NQ) if isinstance(count, int) else count

            def steps(engine, body):
                for t in range(-2, 4):
                    body(t, t % 2, stages(t))
                with engine.Fori(2, PEELED_END // 2) as i:
                    for k in range(2):
                        body(2 * i + k, k, ALL)
                for t in range(PEELED_END, NQ + 2):
                    body(t, t % 2, stages(t))

            with nc.Block() as block:
                LOADS = 16

                @block.sync
                def _(sp):
                    for dst, src in ((tok_w_sb[:, :, :], tok_w), (cols[:, :], columns), (mats_sb[:, :, :], mats),
                                     (wq_sb[:, :], wq), (wk_sb[:, :], wk), (w1_sb[:, :, :], w1), (b1_sb[:, :], b1),
                                     (wr_sb[:, :], wr), (br_sb[:, :, :, :], br), (w2_sb[:, :, :], w2),
                                     (b2_sb[:, :], b2), (sel_sb[:, :, :, :], selectors), (prio[:, :, :, :], priority)):
                        sp.dma_start(dst, src).then_inc(weights_loaded, 16)

                    def load(u, p):
                        wait(sp, tok_done, u - 1)
                        sp.dma_start(xt[p][:, :, :, :], x[u, :, :, :, :]).then_inc(x_ready[p], 16)

                    load(0, 0)
                    load(1, 1)
                    with sp.Fori(1, NQ // 2) as i:
                        for k in range(2):
                            load(2 * i + k, k)

                @block.tensor
                def _(pe):
                    pe.wait_ge(weights_loaded, 16 * 13)
                    nc.tensor.matmul(banks[0][0:D, 0:D], wq_sb[:, :], wk_sb[:, :], start=True, stop=True)
                    nc.tensor.matmul(banks[0][D:P, D:P], wq_sb[:, :], wk_sb[:, :], start=True, stop=True)
                    for e in range(E):
                        nc.tensor.matmul(banks[1][:, e:e + 1], w1_sb[0:D, e, :], beta[0:D, :], start=True, stop=True)
                    pe.wait_ge(setup_vec, 2)
                    nc.tensor.matmul(banks[2][0:C, 0:E], beta_rows[:, :], wr_sb[0:D, :], start=True, stop=True)\
                        .then_inc(setup_mm, 1)
                    pe.wait_ge(setup_vec, SETUP_ALL)

                    def embed(c):
                        for half in range(2):
                            last = nc.tensor.matmul(tok_bank[D * half:D * half + D, 0:2 * PATCHES], tok_w_sb[:, c, :],
                                                    xt_now[:, c, half, :], start=(c == 0), stop=(c == KC - 1))
                        return last

                    def body(t, p, has):
                        nonlocal xt_now
                        emb, ln1, att, ln2, choose = has
                        o = 1 - p
                        xt_now = xt[p]

                        def embedding(part):
                            if part == 0:
                                if isinstance(t, int):
                                    pe.wait_ge(x_ready[p], 16 * ((t + 2) // 2 + 1))
                                else:
                                    pe.wait_ge(x_ready[p], 8 * (t - p) + 32)
                                wait(pe, h_ready, t + 2)
                            for c in EMBED[part]:
                                last = embed(c)
                            if part == 3:
                                last.then_inc(tok_done, 1)

                        def scores(q):
                            k, half = q // 2, q % 2
                            if q == 0:
                                pe.wait_ge(z_ready, t + 1)
                            wait(pe, exp_done, 4 * t + q - 1)
                            a, b = D * half, D * half + D
                            for c in range(2):
                                s = k * N + START[c]
                                last = nc.tensor.matmul(s_bank[half][0:C, c * N:c * N + N], z[p][a:b, s:s + C],
                                                        xn[p][a:b, k * N:k * N + N], start=True, stop=True)
                            last.then_inc(s_done, 1)

                        def transpose_probs(q):
                            half = q % 2
                            pe.wait_ge(probs_ready, 4 * t + q + 1)
                            wait(pe, pT_ready[half], 2 * t + q // 2)
                            for ic in range(2):
                                for jc in range(2):
                                    o0 = jc * N + START[ic]
                                    last = nc.tensor.transpose(pT_bank[half][0:C, o0:o0 + C],
                                                               probs[half][:, ic, START[jc]:START[jc] + C],
                                                               identity[0:C, 0:C])
                            last.then_inc(pT_done, 1)

                        def weigh(k):
                            for half in range(2):
                                pe.wait_ge(pT_ready[half], 2 * t + k + 1)
                            if k == 0:
                                pe.wait_ge(xnT_ready, t + 1)
                                wait(pe, h1_ready, t)
                            for jc in range(2):
                                for half in range(2):
                                    last = nc.tensor.matmul(pv_bank[D * half:D * half + D, k * N:k * N + N],
                                                            xnT[p][0:ROWS[jc], k, jc, D * half:D * half + D],
                                                            probsT[half][0:ROWS[jc], jc, :],
                                                            start=(jc == 0), stop=(jc == 1))
                            last.then_inc(pv_done, 1)

                        if att:
                            scores(0)
                            scores(1)
                        if ln1:
                            pe.wait_ge(h_ready, t + 2)
                            wait(pe, logits_ready, t - 1)
                            nc.tensor.matmul(xc_bank[:, 0:T], center, h[o][:, :], start=True, stop=True)\
                                .then_inc(xc1_done, 1)
                        if ln2:
                            pe.wait_ge(sq2_ready, t)
                            wait(pe, z_ready, last_quad(t + 1))
                            nc.tensor.matmul(var_bank[:, 0:T], mean, stat2[:, :], start=True, stop=True)\
                                .then_inc(var2_done, 1)
                        if emb:
                            embedding(0)
                        if att:
                            transpose_probs(0)
                        if ln1:
                            pe.wait_ge(sq1_ready, t + 2)
                            wait(pe, log2_ready, t)
                            nc.tensor.matmul(var_bank[:, 0:T], mean, stat1[:, :], start=True, stop=True)\
                                .then_inc(var1_done, 1)
                        if att:
                            transpose_probs(1)
                            scores(2)
                            scores(3)
                        if emb:
                            embedding(1)
                        if ln1:
                            pe.wait_ge(xn_ready, t + 2)
                            nc.tensor.matmul(var_bank[:, 0:T], qk_block[:, :], xn[o][:, :], start=True, stop=True)\
                                .then_inc(z_done, 1)
                            wait(pe, pT_ready[1], 2 * t + 1)
                            for k in range(2):
                                for jc in range(2):
                                    s = k * N + START[jc]
                                    c0 = (2 * k + jc) * P
                                    last = nc.tensor.transpose(pT_bank[1][0:C, c0:c0 + P], xn[o][:, s:s + C], identity)
                            last.then_inc(xnT_done, 1)
                        if att:
                            weigh(0)
                        if ln2:
                            pe.wait_ge(xn2_ready, t)
                            wait(pe, xn_ready, last_quad(t + 2))
                            wait(pe, xc1_ready, last_quad(t + 2))
                            if not ln1:
                                wait(pe, logits_ready, t - 1)
                            nc.tensor.matmul(xc_bank[:, 0:T], wr_block[:, :],
                                             xn2[:, :], start=True, stop=True).then_inc(logitsT_done, 1)
                        if emb:
                            embedding(2)
                        if att:
                            transpose_probs(2)
                            if ln1:
                                pe.wait_ge(xnT_ready, t + 2)
                            transpose_probs(3)
                        if ln2:
                            pe.wait_ge(logitsT_ready, t)
                            for n in range(CHUNKS):
                                s = (n // 2) * N + START[n % 2]
                                last = nc.tensor.matmul(xc_bank[0:C, 2 * E * n:2 * E * n + 2 * E], logitsT[:, s:s + C],
                                                        identity[:, 0:2 * E], start=True, stop=True)
                            last.then_inc(logits_done, 1)
                        if emb:
                            embedding(3)
                        if att:
                            weigh(1)

                    xt_now = None
                    steps(pe, body)

                @block.scalar
                def _(act):
                    act.preload_act_table_set("natural_log_exp_and_others")
                    act.wait_ge(setup_vec, SETUP_ALL)

                    def body(t, p, has):
                        emb, ln1, att, ln2, choose = has
                        o = 1 - p

                        def exps(q):
                            half = q % 2
                            act.wait_ge(nmax_ready, 4 * t + q + 1)
                            wait(act, pT_done, 4 * t + q - 1)
                            for c in range(2):
                                last = nc.scalar.activation(probs[half][:, c, :], s_bank[half][0:C, c * N:c * N + N],
                                                            ACT.Exp, bias=nmax[:, q, c:c + 1],
                                                            accum_out=psums[:, q, c:c + 1])
                            last.then_inc(exp_done, 1)

                        def take_probsT(q):
                            act.wait_ge(pT_done, 4 * t + q + 1)
                            wait(act, pv_done, 2 * t + q // 2)
                            nc.scalar.copy(probsT[0][:, :, :], pT_bank[0][0:C, 0:T].rearrange("p (c n) -> p c n", c=2))\
                                .then_inc(pT_ready[0], 1)

                        if att:
                            exps(0)
                            exps(1)
                        if ln1:
                            act.wait_ge(xc1_done, t + 2)
                            wait(act, xn_ready, t + 1)
                            nc.scalar.activation(stat1[:, :], xc_bank[:, 0:T], ACT.Square).then_inc(sq1_ready, 1)
                        if ln2:
                            act.wait_ge(var2_done, t)
                            nc.scalar.activation(stat2[:, :], var_bank[:, 0:T], ACT.Ln, bias=eps2[:, :], scale=1.0 + EPS)\
                                .then_inc(log2_ready, 1)
                        if ln2:
                            act.wait_ge(log2_ready, t)
                            nc.scalar.activation(stat2[:, :], stat2[:, :], ACT.Exp, scale=-0.5)\
                                .then_inc(rstd2_ready, 1)
                        if ln1:
                            wait(act, xc2_ready, t)
                            nc.scalar.copy(xc1[o][:, :], xc_bank[:, 0:T]).then_inc(xc1_ready, 1)
                        if att:
                            take_probsT(0)
                        if ln1:
                            act.wait_ge(var1_done, t + 2)
                            nc.scalar.activation(stat1[:, :], var_bank[:, 0:T], ACT.Ln, bias=eps1[:, :])\
                                .then_inc(log1_ready, 1)
                            act.wait_ge(log1_ready, t + 2)
                            nc.scalar.activation(stat1[:, :], stat1[:, :], ACT.Exp, scale=-0.5)\
                                .then_inc(rstd1_ready, 1)
                        if choose:
                            act.wait_ge(router_vec, VEC * (t - 2) + 12)
                            nc.scalar.activation(exp_gap[:, :, :], gap[:, :, :], ACT.Exp, scale=-1.0)\
                                .then_inc(exp_gap_ready, 1)
                        if att:
                            exps(2)
                            exps(3)
                        if ln2:
                            act.wait_ge(logitsT_done, t)
                            wait(act, logits_done, t - 1)
                            nc.scalar.copy(logitsT[:, :], xc_bank[:, 0:T]).then_inc(logitsT_ready, 1)
                        if att:
                            take_probsT(2)
                        if emb:
                            act.wait_ge(tok_done, t + 3)
                            wait(act, h_kept, t + 1)
                            nc.scalar.activation(h[p][:, :].rearrange("p (k n) -> p k n", k=2)[:, :, 1:N],
                                                 tok_bank[:, 0:2 * PATCHES].rearrange("p (k n) -> p k n", k=2),
                                                 ACT.Identity, bias=tok_b).then_inc(h_ready, 1)
                        if att:
                            act.wait_ge(xc2_ready, t + 1)
                            wait(act, xn2_ready, t)
                            nc.scalar.activation(stat2[:, :], xc2[:, :], ACT.Square).then_inc(sq2_ready, 1)

                    steps(act, body)

                @block.vector
                def _(dve):
                    count = [0]

                    def wide(column):
                        return column[:, :, :].unsqueeze(3).to_broadcast(WIDE)

                    def done(instruction):
                        count[0] += 1
                        instruction.then_inc(setup_vec, 1)
                        dve.wait_ge(setup_vec, count[0])

                    dve.wait_ge(weights_loaded, 16 * 13)
                    done(nc.vector.memset(eps1[:, :], EPS))
                    done(nc.vector.tensor_copy(beta_rows[:, :], beta[0:D, :].to_broadcast([D, C])))
                    done(nc.vector.memset(eps2[:, :], EPS * EPS))
                    done(nc.vector.memset(qk_block[:, :], 0.0))
                    done(nc.vector.memset(wr_block[:, :], 0.0))
                    for p in range(2):
                        done(nc.vector.tensor_copy(h[p][:, :].rearrange("p (k n) -> p k n", k=2)[:, :, 0],
                                                   cls_tok.to_broadcast([P, 2])))
                    dve.wait_ge(setup_mm, 1)
                    nc.vector.tensor_tensor(b1_full[:, :], banks[1][:, 0:E], b1_sb[:, :], ALU.add)
                    nc.vector.tensor_tensor(br_full[0:C, :, :, :].rearrange("p c a e -> p (c a) e"),
                                            br_sb[0:C, :, :, :].rearrange("p c a e -> p (c a) e"),
                                            banks[2][0:C, 0:E].unsqueeze(1).to_broadcast([C, 2 * CHUNKS, E]), ALU.add)
                    for half in range(2):
                        a, b = D * half, D * half + D
                        nc.vector.tensor_scalar(qk_block[a:b, a:b], banks[0][a:b, a:b], float(D) ** -0.5, None, ALU.mult)
                        nc.vector.tensor_scalar(wr_block[a:b, half * E:half * E + E], wr_sb[a:b, :], gamma[a:b, :], None, ALU.mult)
                    nc.vector.tensor_copy(sel_r[:, :, :, :], sel_sb[:, :, :, :])
                    nc.vector.tensor_copy(b2_hi[:, :], b2_sb[:, :])
                    done(nc.vector.tensor_scalar(w1_sb[:, :, :], w1_sb[:, :, :], gamma, None, ALU.mult))
                    done(nc.vector.tensor_copy(w1_hi[:, :, :], w1_sb[:, :, :]))
                    nc.vector.tensor_tensor(b2_lo[:, :], b2_sb[:, :], b2_hi[:, :].bitcast(f32), ALU.subtract)
                    done(nc.vector.tensor_tensor(w1_lo[:, :, :], w1_sb[:, :, :], w1_hi[:, :, :].bitcast(f32), ALU.subtract))
                    assert count[0] == SETUP_ALL

                    def body(t, p, has):
                        emb, ln1, att, ln2, choose = has
                        o = 1 - p

                        def maxima(q):
                            half = q % 2
                            dve.wait_ge(s_done, 4 * t + q + 1)
                            nc.vector.tensor_reduce(nmax[:, q, :], s_bank[half][0:C, 0:T].rearrange("p (c n) -> p c n", c=2),
                                                    axis=AX.X, op=ALU.max, negate=True).then_inc(nmax_ready, 1)

                        def reciprocals(q):
                            dve.wait_ge(exp_done, 4 * t + q + 1)
                            nc.vector.reciprocal(rsums[:, q, :], psums[:, q, :]).then_inc(rsum_ready, 1)

                        def take_probsT(q):
                            dve.wait_ge(pT_done, 4 * t + q + 1)
                            wait(dve, pv_done, 2 * t + q // 2)
                            nc.vector.tensor_copy(probsT[1][:, :, :],
                                                  pT_bank[1][0:C, 0:T].rearrange("p (c n) -> p c n", c=2))\
                                .then_inc(pT_ready[1], 1)

                        def choice(first_step, end):
                            if not choose:
                                return
                            for r in range(first_step, end):
                                if r == 0:
                                    dve.wait_ge(logits_ready, t - 1)
                                elif r != 12:
                                    dve.wait_ge(router_vec, VEC * (t - 2) + r)
                                if r == 0:
                                    step = nc.vector.tensor_reduce(top1[:, :, :], logits[:, :, :, :], axis=AX.X, op=ALU.max)
                                elif r == 1:
                                    step = nc.vector.tensor_tensor(is_max[:, :, :, :], logits[:, :, :, :], wide(top1), ALU.is_equal)
                                elif r == 2:
                                    step = nc.vector.tensor_tensor(ranked[:, :, :, :], is_max[:, :, :, :], prio[0:C, :, :, :], ALU.mult)
                                elif r == 3:
                                    step = nc.vector.tensor_reduce(best[:, :, :], ranked[:, :, :, :], axis=AX.X, op=ALU.max)
                                elif r == 4:
                                    wait(dve, router_pool, POOL * (t - 2))
                                    step = nc.vector.tensor_tensor(first[:, :, :, :], ranked[:, :, :, :], wide(best), ALU.is_equal)
                                elif r == 5:
                                    step = nc.vector.scalar_tensor_tensor(rest[:, :, :, :], first[:, :, :, :], -3.0e38,
                                                                          logits[:, :, :, :], ALU.mult, ALU.add)
                                elif r == 6:
                                    step = nc.vector.tensor_reduce(top2[:, :, :], rest[:, :, :, :], axis=AX.X, op=ALU.max)
                                elif r == 7:
                                    step = nc.vector.tensor_tensor(is_max[:, :, :, :], rest[:, :, :, :], wide(top2), ALU.is_equal)
                                elif r == 8:
                                    step = nc.vector.tensor_tensor(ranked[:, :, :, :], is_max[:, :, :, :], prio[0:C, :, :, :], ALU.mult)
                                elif r == 9:
                                    step = nc.vector.tensor_reduce(best[:, :, :], ranked[:, :, :, :], axis=AX.X, op=ALU.max)
                                elif r == 10:
                                    step = nc.vector.tensor_tensor(second[:, :, :, :], ranked[:, :, :, :], wide(best), ALU.is_equal)
                                elif r == 11:
                                    step = nc.vector.tensor_tensor(gap[:, :, :], top1[:, :, :], top2[:, :, :], ALU.subtract)
                                elif r == 12:
                                    dve.wait_ge(exp_gap_ready, t - 1)
                                    step = nc.vector.tensor_scalar(sum_exp[:, :, :], exp_gap[:, :, :], 1.0, None, ALU.add)
                                elif r == 13:
                                    step = nc.vector.reciprocal(weight1[:, :, :], sum_exp[:, :, :])
                                elif r == 14:
                                    step = nc.vector.tensor_tensor(weight2[:, :, :], exp_gap[:, :, :], weight1[:, :, :], ALU.mult)
                                step.then_inc(router_vec, 1)

                        if att:
                            maxima(0)
                            maxima(1)
                        choice(0, 2)
                        if ln2:
                            dve.wait_ge(h_kept, t)
                            nc.vector.tensor_tensor(h1_store[:, t - 1, :], pv_bank[:, 0:T], h1_store[:, t - 1, :], ALU.add)\
                                .then_inc(h1_ready, 1)
                        choice(2, 4)
                        if att:
                            reciprocals(0)
                        choice(4, 6)
                        if att:
                            reciprocals(1)
                        if ln2:
                            dve.wait_ge(rstd2_ready, t)
                            wait(dve, xn2_kept, t - 1)
                            wait(dve, logitsT_done, t - 1)
                            nc.vector.tensor_tensor(xn2[:, :], xc2[:, :], stat2[:, :], ALU.mult).then_inc(xn2_ready, 1)
                        choice(6, 9)
                        if att:
                            maxima(2)
                        choice(9, 10)
                        if ln1:
                            dve.wait_ge(rstd1_ready, t + 2)
                            nc.vector.tensor_tensor(xn[o][:, :], xc_bank[:, 0:T], stat1[:, :], ALU.mult)\
                                .then_inc(xn_ready, 1)
                        choice(10, 11)
                        if att:
                            maxima(3)
                        choice(11, 12)
                        if att:
                            take_probsT(1)
                        choice(12, 15)
                        if ln1:
                            dve.wait_ge(z_done, t + 2)
                            nc.vector.tensor_copy(z[o][:, :], var_bank[:, 0:T]).then_inc(z_ready, 1)
                        if att:
                            reciprocals(2)
                        if ln1:
                            dve.wait_ge(xnT_done, t + 2)
                            nc.vector.tensor_copy(xnT[o][:, :, :, :],
                                                  pT_bank[1][0:C, :].rearrange("p (k j d) -> p k j d", k=2, j=2))\
                                .then_inc(xnT_ready, 1)
                        if att:
                            reciprocals(3)
                            take_probsT(3)
                        if ln2:
                            dve.wait_ge(logits_done, t)
                            nc.vector.tensor_tensor(logits[:, :, :, :],
                                                    xc_bank[0:C, 0:2 * E * CHUNKS].rearrange("p (c a e) -> p c a e", a=2, e=E),
                                                    br_full[0:C, :, :, :], ALU.add).then_inc(logits_ready, 1)
                        if att:
                            dve.wait_ge(pv_done, 2 * t + 2)
                            wait(dve, sq2_ready, t)
                            nc.vector.tensor_tensor(xc2[:, :], pv_bank[:, 0:T], xc1[p][:, :], ALU.add)\
                                .then_inc(xc2_ready, 1)

                    steps(dve, body)

                @block.gpsimd
                def _(pool):
                    def wide(column):
                        return column[:, :, :].unsqueeze(3).to_broadcast(WIDE)

                    def body(t, p, has):
                        emb, ln1, att, ln2, choose = has
                        def normalize(q):
                            half = q % 2
                            pool.wait_ge(rsum_ready, 4 * t + q + 1)
                            nc.gpsimd.tensor_tensor(probs[half][:, :, :], probs[half][:, :, :],
                                                    rsums[:, q, :].unsqueeze(2).to_broadcast([C, 2, N]), ALU.mult)\
                                .then_inc(probs_ready, 1)

                        if ln1:
                            pool.wait_ge(h_ready, t + 2)
                            nc.gpsimd.tensor_copy(h1_store[:, t + 1, :], h[1 - p][:, :]).then_inc(h_kept, 1)
                        if att:
                            normalize(0)
                            normalize(1)
                        if ln2:
                            pool.wait_ge(xn2_ready, t)
                            nc.gpsimd.tensor_copy(xn2_store[:, t - 1, :], xn2[:, :]).then_inc(xn2_kept, 1)
                        if att:
                            normalize(2)
                            normalize(3)
                        if choose:
                            b = POOL * (t - 2)
                            pool.wait_ge(router_vec, VEC * (t - 2) + VEC)
                            nc.gpsimd.tensor_tensor(part_a[:, :, :, :], first[:, :, :, :], wide(weight1), ALU.mult)\
                                .then_inc(router_pool, 1)
                            nc.gpsimd.tensor_tensor(part_b[:, :, :, :], second[:, :, :, :], wide(weight2), ALU.mult)\
                                .then_inc(router_pool, 1)
                            pool.wait_ge(router_pool, b + 2)
                            nc.gpsimd.tensor_tensor(w_store[:, t - 2, :, :, :], part_a[:, :, :, :], part_b[:, :, :, :], ALU.add)\
                                .then_inc(router_pool, 1)

                    steps(pool, body)

        part2 = ExitStack()
        with part2:
            def sb2(name, shape, dt=f32):
                return part2.enter_context(nc.sbuf_tensor(name, shape, dt))

            x2 = [[sb2(f"x2_{p}{half}", [P, T], f32r) for half in range(2)] for p in range(2)]
            gelu = [[sb2(f"gelu{b}{half}", [P, T]) for half in range(2)] for b in range(2)]
            scaled = [[sb2(f"scaled{b}{half}", [P, T]) for half in range(2)] for b in range(2)]
            w_now = [sb2(f"w_now{p}", [C, CHUNKS, 2, 2, E]) for p in range(2)]
            wT = [sb2(f"wT{p}", [S, T], f32r) for p in range(2)]
            result = [sb2(f"result{p}", [P, T]) for p in range(2)]

            z1_bank = banks[0:2]
            wb_bank = banks[2:4]
            y_bank = banks[4:6]
            wT_bank = banks[6:8]

            x2_hi_ready, x2_lo_ready = sem("x2_hi_ready"), sem("x2_lo_ready")
            w_hi_ready, w_lo_ready = sem("w_hi_ready"), sem("w_lo_ready")
            wT_done, wT_ready = sem("wT_done"), sem("wT_ready")
            z1_done = sem("z1_done")
            gelu_ready = sem("gelu_ready")
            wb_done = sem("wb_done")
            scaled_ready = sem("scaled_ready")
            y_done = sem("y_done")
            result_ready = sem("result_ready")
            out_stored = [sem("out_stored0"), sem("out_stored1")]

            def quads(engine, body):
                body(0, 0, True, True)
                body(1, 1, True, True)
                with engine.Fori(1, NQ // 2 - 1) as i:
                    for k in range(2):
                        body(2 * i + k, k, True, True)
                body(NQ - 2, 0, True, False)
                body(NQ - 1, 1, False, False)

            with nc.Block() as block:

                @block.tensor
                def _(pe):
                    def first_layer(u, p, e):
                        if e == 0:
                            pe.wait_ge(x2_hi_ready, 2 * u + 2)
                            pe.wait_ge(x2_lo_ready, 2 * u + 2)
                        for half in range(2):
                            wait(pe, gelu_ready, 16 * u + 2 * e + half - 1)
                            nc.tensor.matmul(z1_bank[half][:, 0:T], w1_hi[:, e, :], x2[p][half][:, :], start=True, stop=False)
                            nc.tensor.matmul(z1_bank[half][:, 0:T], w1_lo[:, e, :], x2[p][half][:, :], start=False, stop=True)\
                                .then_inc(z1_done, 1)

                    def spread_weights(u, p, e):
                        if e == 0:
                            pe.wait_ge(wT_ready, u + 1)
                        for half in range(2):
                            wait(pe, scaled_ready, 16 * u + 2 * e + half - 1)
                            nc.tensor.matmul(wb_bank[half][:, 0:T], sel_r[:, half, e, :], wT[p][:, :], start=True, stop=True)\
                                .then_inc(wb_done, 1)

                    def second_layer(u, p, e):
                        if e == 0:
                            wait(pe, result_ready, u - 1)
                            nc.tensor.matmul(y_bank[p][:, 0:T], b2_hi[:, :], wT[p][:, :], start=True, stop=False)
                            nc.tensor.matmul(y_bank[p][:, 0:T], b2_lo[:, :], wT[p][:, :], start=False, stop=False)
                        pe.wait_ge(scaled_ready, 16 * u + 2 * e + 2)
                        for half in range(2):
                            last = nc.tensor.matmul(y_bank[p][D * half:D * half + D, 0:T], w2_sb[:, e, :],
                                                    scaled[e % 2][half][:, :], start=False, stop=(e == E - 1))
                        if e == E - 1:
                            last.then_inc(y_done, 1)

                    def transpose_weights(u, p):
                        pe.wait_ge(w_lo_ready, u + 1)
                        wait(pe, wT_ready, u - 1)
                        for n in range(CHUNKS):
                            s = (n // 2) * N + START[n % 2]
                            last = nc.tensor.transpose(wT_bank[p][0:S, s:s + C], w_now[p][:, n, :, :, :].rearrange("p a h e -> p (a h e)"),
                                                       identity[0:C, 0:C])
                        last.then_inc(wT_done, 1)

                    def body(u, p, has_next, _):
                        for e in range(E):
                            last_step = e == E - 1
                            if not last_step:
                                first_layer(u, p, e + 1)
                            elif has_next:
                                first_layer(u + 1, 1 - p, 0)
                            if e == 4 and has_next:
                                transpose_weights(u + 1, 1 - p)
                            if not last_step:
                                spread_weights(u, p, e + 1)
                            elif has_next:
                                spread_weights(u + 1, 1 - p, 0)
                            second_layer(u, p, e)

                    first_layer(0, 0, 0)
                    transpose_weights(0, 0)
                    spread_weights(0, 0, 0)
                    quads(pe, body)

                @block.scalar
                def _(act):
                    act.preload_act_table_set("gelu_and_others")

                    def split_hi(u, p):
                        wait(act, z1_done, 16 * u - 16)
                        for half in range(2):
                            a, b = D * half, D * half + D
                            nc.scalar.copy(x2[p][half][a:b, :], xn2_store[a:b, u, :]).then_inc(x2_hi_ready, 1)

                    def fetch_weights(u, p):
                        wait(act, wT_done, u - 1)
                        nc.scalar.copy(w_now[p][:, :, :, 0, :].bitcast(f32r), w_store[:, u, :, :, :]).then_inc(w_hi_ready, 1)

                    def take_wT(u, p):
                        act.wait_ge(wT_done, u + 1)
                        wait(act, y_done, u - 1)
                        nc.scalar.copy(wT[p][:, :], wT_bank[p][0:S, 0:T]).then_inc(wT_ready, 1)

                    def body(u, p, has_next, has_after_next):
                        for e in range(E):
                            for half in range(2):
                                n = 16 * u + 2 * e + half
                                act.wait_ge(z1_done, n + 1)
                                wait(act, scaled_ready, n - 3)
                                nc.scalar.activation(gelu[e % 2][half][:, :], z1_bank[half][:, 0:T], ACT.Gelu,
                                                     bias=b1_full[:, e:e + 1]).then_inc(gelu_ready, 1)
                            if e == 5 and has_next:
                                take_wT(u + 1, 1 - p)
                        if has_after_next:
                            split_hi(u + 2, p)
                            fetch_weights(u + 2, p)

                    split_hi(0, 0)
                    fetch_weights(0, 0)
                    take_wT(0, 0)
                    split_hi(1, 1)
                    fetch_weights(1, 1)
                    quads(act, body)

                @block.vector
                def _(dve):
                    def finish(u, p):
                        dve.wait_ge(y_done, u + 1)
                        if isinstance(u, int):
                            wait(dve, out_stored[p], 16 * (u // 2))
                        else:
                            dve.wait_ge(out_stored[p], 8 * (u - p))
                        nc.vector.tensor_tensor(result[p][:, :], y_bank[p][:, 0:T], h1_store[:, u, :], ALU.add)\
                            .then_inc(result_ready, 1)

                    def weights_lo(u, p):
                        dve.wait_ge(w_hi_ready, u + 1)
                        nc.vector.tensor_tensor(w_now[p][:, :, :, 1, :], w_store[:, u, :, :, :], w_now[p][:, :, :, 0, :],
                                                ALU.subtract).then_inc(w_lo_ready, 1)

                    def body(u, p, has_next, _):
                        for e in range(E):
                            if e == 2 and has_next:
                                weights_lo(u + 1, 1 - p)
                            for half in range(2):
                                n = 16 * u + 2 * e + half
                                dve.wait_ge(gelu_ready, n + 1)
                                dve.wait_ge(wb_done, n + 1)
                                nc.vector.tensor_tensor(scaled[e % 2][half][:, :], wb_bank[half][:, 0:T],
                                                        gelu[e % 2][half][:, :], ALU.mult).then_inc(scaled_ready, 1)
                            if e == 0 and not (isinstance(u, int) and u == 0):
                                finish(u - 1, 1 - p)

                    weights_lo(0, 0)
                    quads(dve, body)
                    finish(NQ - 1, 1)

                @block.gpsimd
                def _(pool):
                    def split_lo(u, p):
                        for half in range(2):
                            a, b = D * half, D * half + D
                            c, d = D * (1 - half), D * (1 - half) + D
                            pool.wait_ge(x2_hi_ready, 2 * u + half + 1)
                            if half:
                                pool.wait_ge(x2_lo_ready, 2 * u + 1)
                            nc.gpsimd.tensor_tensor(x2[p][half][c:d, :], xn2_store[a:b, u, :],
                                                    x2[p][half][a:b, :].bitcast(f32), ALU.subtract)\
                                .then_inc(x2_lo_ready, 1)

                    def body(u, p, has_next, has_after_next):
                        if has_after_next:
                            split_lo(u + 2, p)

                    split_lo(0, 0)
                    split_lo(1, 1)
                    quads(pool, body)

                @block.sync
                def _(sp):
                    def body(u, p, *_):
                        sp.wait_ge(result_ready, u + 1)
                        sp.dma_start(out[u, :, :], result[p][:, :]).then_inc(out_stored[p], 16)

                    quads(sp, body)
                    for p in range(2):
                        sp.wait_ge(out_stored[p], 16 * (NQ // 2))


SETUP_ALL = 10


def kernel(**inputs):
    import numpy as np
    import concourse.bacc as bacc
    from concourse import mybir
    from concourse.bass_utils import run_bass_kernel_spmd

    a = {k: np.asarray(v) for k, v in inputs.items()}
    PATCH, PARTS = 16, 128
    B, CH, H, W = a["x"].shape
    nh, nw = H // PATCH, W // PATCH
    D = a["L0_tok_W"].shape[0]
    E = a["L0_ffn_W1"].shape[0]
    NQ = B // 4
    rows = PARTS // PATCH
    chunks = PATCH // rows

    x = a["x"].reshape(NQ, 2, 2, CH, nh, chunks, rows, nw, PATCH).transpose(0, 6, 8, 3, 5, 1, 2, 4, 7)
    x = np.ascontiguousarray(x).reshape(NQ, PARTS, CH * chunks, 2, 2 * nh * nw)
    twice = lambda m: np.concatenate([m, m], axis=0)
    arrays = {
        "x": x,
        "tok_w": a["L0_tok_W"].T.reshape(CH * chunks, PARTS, D).transpose(1, 0, 2),
        "columns": twice(np.stack([a["L0_tok_b"], a["cls_tok"].reshape(D), a["L0_ffn_gamma"], a["L0_ffn_beta"]], axis=1)),
        "wq": a["L0_attn_Wq"],
        "wk": a["L0_attn_Wk"],
        "w1": twice(a["L0_ffn_W1"].transpose(1, 0, 2)),
        "b1": a["L0_ffn_b1"].T,
        "wr": twice(a["L0_ffn_Wr"]),
        "br": np.broadcast_to(a["L0_ffn_br"], (PARTS, 4, 2, E)),
        "w2": a["L0_ffn_W2"].transpose(1, 0, 2),
    }
    b2 = np.zeros((2, 2, E, 2, D), np.float32)
    for half in range(2):
        b2[half, :, :, half, :] = a["L0_ffn_b2"]
    arrays["b2"] = b2.reshape(4 * E, 2 * D)
    blocks = np.kron(np.eye(2), np.ones((D, D))) / D
    arrays["mats"] = np.stack([np.eye(PARTS) - blocks, blocks, np.eye(PARTS)], axis=1)
    rows_of = np.zeros((2, 2, E, 2, E))
    for half in range(2):
        rows_of[half, :, :, half, :] = np.eye(E)
    arrays["selectors"] = np.broadcast_to(rows_of.reshape(4 * E, 2, E, 1), (4 * E, 2, E, PARTS))
    arrays["priority"] = np.broadcast_to(np.arange(E, 0, -1), (PARTS, 4, 2, E))

    nc = bacc.Bacc("TRN2", target_bir_lowering=False, num_devices=1)
    feeds, handles = {}, {}
    for name, value in arrays.items():
        feeds[name + "_in"] = np.ascontiguousarray(value, dtype=np.float32)
        handles[name] = nc.dram_tensor(name + "_in", value.shape, mybir.dt.float32, kind="ExternalInput").ap()
    N = nh * nw + 1
    out = nc.dram_tensor("tokens_out", (NQ, PARTS, 2 * N), mybir.dt.float32, kind="ExternalOutput").ap()
    vit_block_program(nc, out=out, **handles)
    got = run_bass_kernel_spmd(nc, [feeds], core_ids=[0]).results[0]["tokens_out"]
    return got.reshape(NQ, 2, D, 2, N).transpose(0, 1, 3, 4, 2).reshape(B, N, D)
```

```python
import concourse.bass as bass
from concourse import mybir
from contextlib import ExitStack


def vit_block_program(nc, x, tok_w, columns, wq, wk, w1, b1, wr, br, w2, b2, mats, selectors, priority, out):
    f32 = mybir.dt.float32
    f32r = mybir.dt.float32r
    ALU = mybir.AluOpType
    ACT = mybir.ActivationFunctionType
    AX = mybir.AxisListType

    P = 128
    NQ = x.shape[0]
    KC = x.shape[2]
    PATCHES = x.shape[4] // 2
    N = PATCHES + 1
    T = 2 * N
    D = P // 2
    E = w1.shape[1]
    C = (N + 1) // 2
    START = (0, N - C)
    ROWS = (N - C, C)
    EPS = 1e-5
    CHUNKS = 4
    S = 4 * E
    BANK = 512

    ctx = ExitStack()
    with ctx:
        def sb(name, shape, dt=f32):
            return ctx.enter_context(nc.sbuf_tensor(name, shape, dt))

        def sem(name):
            return ctx.enter_context(nc.semaphore(name))

        tok_w_sb = sb("tok_w_sb", [P, KC, D])
        cols = sb("cols", [P, 4])
        tok_b, cls_tok, gamma, beta = (cols[:, j:j + 1] for j in range(4))
        mats_sb = sb("mats_sb", [P, 3, P])
        center, mean, identity = (mats_sb[:, j, :] for j in range(3))
        center_r = sb("center_r", [P, P], f32r)
        mean_r = sb("mean_r", [P, P], f32r)
        wq_sb = sb("wq_sb", [D, D])
        wk_sb = sb("wk_sb", [D, D])
        qk_block = sb("qk_block", [P, P])
        w1_hi = sb("w1_hi", [P, E, P], f32r)
        w1_lo = sb("w1_lo", [P, E, P], f32r)
        b1_sb = sb("b1_sb", [P, E])
        b1_full = sb("b1_full", [P, E])
        wr_sb = sb("wr_sb", [P, E])
        wr_block = sb("wr_block", [P, 2 * E])
        br_sb = sb("br_sb", [P, CHUNKS, 2, E])
        br_full = sb("br_full", [P, CHUNKS, 2, E])
        beta_rows = sb("beta_rows", [D, C])
        w2_sb = sb("w2_sb", [P, E, D])
        b2_sb = sb("b2_sb", [P, E])
        sel_r = sb("sel_r", [S, E, P], f32r)
        prio = sb("prio", [P, CHUNKS, 2, E])
        eps1 = sb("eps1", [P, 1])
        eps2 = sb("eps2", [P, 1])

        h1_store = sb("h1_store", [P, NQ, T])
        xn2_store = sb("xn2_store", [P, NQ, T])
        staging = h1_store[:, :, :].rearrange("p q t -> p (q t)")[:, NQ * T - 2 * E * P:NQ * T]
        w1_sb = staging[:, 0:E * P].rearrange("p (e h) -> p e h", e=E)
        sel_sb = staging[0:S, E * P:2 * E * P].rearrange("p (e h) -> p e h", e=E)
        w_store = sb("w_store", [C, NQ, CHUNKS, 2, E])

        banks = [ctx.enter_context(nc.psum_tensor(f"bank{b}", [P, BANK], f32)) for b in range(8)]

        qk_bank, b1_bank, br_bank = banks[3:6]
        tok_w_loaded, weights_loaded, expert_weights_loaded = (
            sem(name) for name in ("tok_w_loaded", "weights_loaded", "expert_weights_loaded"))
        setup_vec = sem("setup_vec")
        setup_mm = sem("setup_mm")

        def wait(engine, semaphore, count):
            if isinstance(count, int) and count <= 0:
                return
            engine.wait_ge(semaphore, count)

        h_hi = [sb(f"hidden_hi{p}", [P, T], f32r) for p in range(2)]
        h_lo = [sb(f"hidden_lo{p}", [P, T], f32r) for p in range(2)]
        xc1 = [sb(f"xc1_{p}", [P, T]) for p in range(2)]
        xc2 = sb("xc2", [P, T])
        xn2 = sb("xn2", [P, T])
        stat1 = sb("stat1", [P, T])
        stat2 = sb("stat2", [P, T])
        sq1_hi, sq1_lo, sq2_hi, sq2_lo = (sb(name, [P, T], f32r) for name in ("sq1_hi", "sq1_lo", "sq2_hi", "sq2_lo"))
        xn = [sb(f"xn{p}", [P, T]) for p in range(2)]
        z = [sb(f"z{p}", [P, T]) for p in range(2)]
        xnT = [sb(f"xnT{p}", [C, 2, 2, P]) for p in range(2)]
        probs = [sb(f"probs{b}", [C, 2, N]) for b in range(2)]
        probsT = [sb(f"probsT{b}", [C, 2, N]) for b in range(2)]
        nmax = sb("nmax", [C, 4, 2])
        psums = sb("psums", [C, 4, 2])
        rsums = sb("rsums", [C, 4, 2])
        WIDE = [C, CHUNKS, 2, E]
        logits = sb("logits", WIDE)
        rest = sb("rest", WIDE)
        is_max = sb("is_max", WIDE)
        ranked = sb("ranked", WIDE)
        first = sb("first", WIDE)
        second = sb("second", WIDE)
        part_a = sb("part_a", WIDE)
        part_b = sb("part_b", WIDE)
        top1, top2, best, gap, exp_gap, sum_exp, weight1, weight2 = (
            sb(name, [C, CHUNKS, 2]) for name in
            ("top1", "top2", "best", "gap", "exp_gap", "sum_exp", "weight1", "weight2"))

        tok_bank = banks[0]
        xc_bank = banks[1]
        var_bank = banks[2]
        s_bank = banks[3:5]
        pT_bank = banks[5:7]
        pv_bank = banks[7]

        x_ready = [sem("x_ready0"), sem("x_ready1")]
        first_pixels = [sem("first_pixels0"), sem("first_pixels1")]
        PIECE = KC // 3
        tok_done = sem("tok_done")
        h_hi_ready, h_lo_ready = sem("h_hi_ready"), sem("h_lo_ready")
        h_kept = sem("h_kept")
        xc1_done = sem("xc1_done")
        xc1_ready, xc2_ready = sem("xc1_ready"), sem("xc2_ready")
        sq1_ready, sq2_ready = sem("sq1_ready"), sem("sq2_ready")
        sq1_lo_ready, sq2_lo_ready = sem("sq1_lo_ready"), sem("sq2_lo_ready")
        var1_done, var2_done = sem("var1_done"), sem("var2_done")
        log1_ready, log2_ready = sem("log1_ready"), sem("log2_ready")
        rstd1_ready, rstd2_ready = sem("rstd1_ready"), sem("rstd2_ready")
        xn_ready = sem("xn_ready")
        z_done, z_ready = sem("z_done"), sem("z_ready")
        xnT_done, xnT_ready = sem("xnT_done"), sem("xnT_ready")
        s_done = sem("s_done")
        nmax_ready = sem("nmax_ready")
        exp_done = sem("exp_done")
        rsum_ready = sem("rsum_ready")
        probs_ready = [sem("probs_ready0"), sem("probs_ready1")]
        pT_done = sem("pT_done")
        pT_ready = [sem("pT_ready0"), sem("pT_ready1")]
        pv_done = sem("pv_done")
        h1_ready = sem("h1_ready")
        xn2_ready = sem("xn2_ready")
        xn2_kept = sem("xn2_kept")
        logits_done = sem("logits_done")
        logits_ready = sem("logits_ready")
        router_vec = sem("router_vec")
        exp_gap_ready = sem("exp_gap_ready")
        router_pool = sem("router_pool")
        VEC = 15
        POOL = 3

        def stages(t):
            return [0 <= t + d < NQ for d in (2, 1, 0, -1, -2)]

        ALL = [True] * 5
        PEELED_END = NQ - 2
        UNROLL = 4
        LOOP_START = 4 + (PEELED_END - 4) % UNROLL
        EMBED = (range(0, 2), range(2, 3), range(3, 4), range(4, KC))

        def last_quad(count):
            return min(count, NQ) if isinstance(count, int) else count

        def steps(engine, step, before={}):
            for t in range(-2, LOOP_START):
                before.get(t, lambda: None)()
                step(t, t % 2, stages(t))
            with engine.Fori(0, (PEELED_END - LOOP_START) // UNROLL) as i:
                for k in range(UNROLL):
                    step(UNROLL * i + LOOP_START + k, k % 2, ALL)
            for t in range(PEELED_END, NQ + 2):
                before.get(t, lambda: None)()
                step(t, t % 2, stages(t))

        with ExitStack() as pixels:
            xt = [pixels.enter_context(nc.sbuf_tensor(f"xt{p}", [P, KC, 2, 2 * PATCHES], f32)) for p in range(2)]

        x2 = [[sb(f"x2_{p}{half}", [P, T], f32r) for half in range(2)] for p in range(2)]
        gelu = [[sb(f"gelu{b}{half}", [P, T]) for half in range(2)] for b in range(4)]
        weighted = [sb(f"weighted{b}", [P, T]) for b in range(2)]
        w_now = [sb(f"w_now{p}", [C, CHUNKS, 2, 2, E]) for p in range(2)]
        wT = [sb(f"wT{p}", [S, T], f32r) for p in range(2)]
        wb = [sb(f"wb{b}", [P, T]) for b in range(2)]
        result = [sb(f"result{p}", [P, T]) for p in range(2)]

        z1_bank = [banks[0:2], banks[2:4]]
        y_bank = banks[4:6]
        spread_bank = banks[6:8]

        x2_hi_ready, x2_lo_ready = sem("x2_hi_ready"), sem("x2_lo_ready")
        w_hi_ready, w_lo_ready = sem("w_hi_ready"), sem("w_lo_ready")
        wT_done, wT_ready = sem("wT_done"), sem("wT_ready")
        z1_done = sem("z1_done")
        gelu_ready = sem("gelu_ready")
        wb_done, wb_ready = sem("wb_done"), sem("wb_ready")
        y_done = sem("y_done")
        weighted_ready = sem("weighted_ready")
        sum_ready = sem("sum_ready")
        out_stored = [sem("out_stored0"), sem("out_stored1")]

        TURN_WT = E // 2

        def turn(e):
            return e if e < TURN_WT else e + 1

        def quads(engine, quad):
            first = 2 + (NQ - 4) % UNROLL
            for u in range(first):
                quad(u, u % 2, True, True)
            with engine.Fori(0, (NQ - 2 - first) // UNROLL) as i:
                for k in range(UNROLL):
                    quad(UNROLL * i + first + k, k % 2, True, True)
            quad(NQ - 2, 0, True, False)
            quad(NQ - 1, 1, False, False)

        with nc.Block() as block:

            @block.sync
            def _(sp):
                def load(u, p):
                    wait(sp, tok_done, u - 1)
                    sp.dma_start(xt[p][:, :, :, :], x[u, :, :, :, :]).then_inc(x_ready[p], 16)

                for dst, src in ((tok_w_sb[:, :, :], tok_w), (cols[:, :], columns)):
                    sp.dma_start(dst, src).then_inc(tok_w_loaded, 16)
                for piece, done in enumerate((*first_pixels, x_ready[0])):
                    c = PIECE * piece
                    sp.dma_start(xt[0][:, c:c + PIECE, :, :], x[0, :, c:c + PIECE, :, :]).then_inc(done, 16)
                for dst, src in ((wq_sb[:, :], wq), (wk_sb[:, :], wk), (wr_sb[:, :], wr), (mats_sb[:, :, :], mats),
                                 (br_sb[:, :, :, :], br), (b1_sb[:, :], b1), (w1_sb[:, :, :], w1)):
                    sp.dma_start(dst, src).then_inc(weights_loaded, 16)
                load(1, 1)
                for dst, src in ((prio[:, :, :, :], priority), (w2_sb[:, :, :], w2), (b2_sb[:, :], b2),
                                 (sel_sb[:, :, :], selectors)):
                    sp.dma_start(dst, src).then_inc(expert_weights_loaded, 16)
                with sp.Fori(1, NQ // 2) as i:
                    for k in range(2):
                        load(2 * i + k, k)

                def quad(u, p, *_):
                    sp.wait_ge(sum_ready, 8 * u + 8)
                    sp.dma_start(out[u, :, :], result[p][:, :]).then_inc(out_stored[p], 16)

                quads(sp, quad)
                for p in range(2):
                    sp.wait_ge(out_stored[p], 16 * (NQ // 2))

            @block.tensor
            def _(pe):
                def set_up():
                    pe.wait_ge(weights_loaded, 16 * 7)
                    nc.tensor.matmul(qk_bank[0:D, 0:D], wq_sb[:, :], wk_sb[:, :], start=True, stop=True)
                    nc.tensor.matmul(qk_bank[D:P, D:P], wq_sb[:, :], wk_sb[:, :], start=True, stop=True)
                    pe.wait_ge(setup_vec, SETUP_COLUMNS)
                    nc.tensor.matmul(br_bank[0:C, 0:E], beta_rows[:, :], wr_sb[0:D, :], start=True, stop=True)\
                        .then_inc(setup_mm, 1)
                    pe.wait_ge(setup_vec, SETUP_ATTENTION)

                def first_biases():
                    for e in range(E):
                        last = nc.tensor.matmul(b1_bank[:, e:e + 1], w1_sb[0:D, e, :], beta[0:D, :], start=True, stop=True)
                    last.then_inc(setup_mm, 1)

                def embed(c):
                    for half in range(2):
                        last = nc.tensor.matmul(tok_bank[D * half:D * half + D, 0:2 * PATCHES], tok_w_sb[:, c, :],
                                                xt_now[:, c, half, :], start=(c == 0), stop=(c == KC - 1))
                    return last

                def step(t, p, has):
                    nonlocal xt_now
                    emb, ln1, att, ln2, choose = has
                    o = 1 - p
                    xt_now = xt[p]
                    late = isinstance(t, int) and t == -1

                    def embedding(part):
                        if isinstance(t, int) and t == -2:
                            if part == 0:
                                pe.wait_ge(tok_w_loaded, 16 * 2)
                        elif part == 0:
                            if isinstance(t, int):
                                pe.wait_ge(x_ready[p], 16 * ((t + 2) // 2 + 1))
                            else:
                                pe.wait_ge(x_ready[p], 8 * (t - p) + 32)
                            wait(pe, h_lo_ready, t + 2)
                        for c in EMBED[part]:
                            if isinstance(t, int) and t == -2 and c % PIECE == 0:
                                pe.wait_ge((*first_pixels, x_ready[0])[c // PIECE], 16)
                            last = embed(c)
                        if part == 3:
                            last.then_inc(tok_done, 1)

                    def scores(k):
                        if k == 0:
                            pe.wait_ge(z_ready, t + 1)
                        wait(pe, exp_done, 4 * t + 2 * k)
                        for c in range(2):
                            s = k * N + START[c]
                            for half in range(2):
                                a, b = D * half, D * half + D
                                last = nc.tensor.matmul(s_bank[half][0:C, c * N:c * N + N], z[p][a:b, s:s + C],
                                                        xn[p][a:b, k * N:k * N + N], start=True, stop=True)
                                if c == 1:
                                    last.then_inc(s_done, 1)

                    def transpose_probs(q):
                        half = q % 2
                        pe.wait_ge(probs_ready[half], 2 * t + q // 2 + 1)
                        wait(pe, pT_ready[half], 2 * t + q // 2)
                        for ic in range(2):
                            for jc in range(2):
                                o0 = jc * N + START[ic]
                                last = nc.tensor.transpose(pT_bank[half][0:C, o0:o0 + C],
                                                           probs[half][:, ic, START[jc]:START[jc] + C],
                                                           identity[0:C, 0:C])
                        last.then_inc(pT_done, 1)

                    def weigh(k):
                        for half in range(2):
                            pe.wait_ge(pT_ready[half], 2 * t + k + 1)
                        if k == 0:
                            pe.wait_ge(xnT_ready, t + 1)
                            wait(pe, h1_ready, t)
                        for jc in range(2):
                            for half in range(2):
                                last = nc.tensor.matmul(pv_bank[D * half:D * half + D, k * N:k * N + N],
                                                        xnT[p][0:ROWS[jc], k, jc, D * half:D * half + D],
                                                        probsT[half][0:ROWS[jc], jc, :],
                                                        start=(jc == 0), stop=(jc == 1))
                        last.then_inc(pv_done, 1)

                    if att:
                        scores(0)
                    if ln1:
                        pe.wait_ge(h_lo_ready, t + 2)
                        wait(pe, logits_ready, t - 1)
                        nc.tensor.matmul(xc_bank[:, 0:T], center_r[:, :], h_hi[o][:, :], start=True, stop=False)
                        nc.tensor.matmul(xc_bank[:, 0:T], center_r[:, :], h_lo[o][:, :], start=False, stop=True)\
                            .then_inc(xc1_done, 1)
                    if late:
                        first_biases()
                    if emb and not late:
                        embedding(0)
                    if ln2:
                        pe.wait_ge(sq2_lo_ready, t)
                        wait(pe, xnT_ready, last_quad(t + 1))
                        nc.tensor.matmul(var_bank[:, 0:T], mean_r[:, :], sq2_hi[:, :], start=True, stop=False)
                        nc.tensor.matmul(var_bank[:, 0:T], mean_r[:, :], sq2_lo[:, :], start=False, stop=True)\
                            .then_inc(var2_done, 1)
                    if emb and not late:
                        embedding(1)
                    if att and not ln1:
                        scores(1)
                    if att:
                        transpose_probs(0)
                    if ln1:
                        pe.wait_ge(sq1_lo_ready, t + 2)
                        wait(pe, log2_ready, t)
                        nc.tensor.matmul(var_bank[:, 0:T], mean_r[:, :], sq1_hi[:, :], start=True, stop=False)
                        nc.tensor.matmul(var_bank[:, 0:T], mean_r[:, :], sq1_lo[:, :], start=False, stop=True)\
                            .then_inc(var1_done, 1)
                    if att:
                        if ln1:
                            scores(1)
                        transpose_probs(1)
                    if emb and not late:
                        embedding(2)
                    if ln1:
                        pe.wait_ge(xn_ready, t + 2)
                        nc.tensor.matmul(var_bank[:, 0:T], qk_block[:, :], xn[o][:, :], start=True, stop=True)\
                            .then_inc(z_done, 1)
                    if att:
                        weigh(0)
                    if emb and not late:
                        embedding(3)
                    if att:
                        transpose_probs(2)
                        transpose_probs(3)
                    if ln1:
                        pe.wait_ge(z_ready, t + 2)
                        for k in range(2):
                            for jc in range(2):
                                s = k * N + START[jc]
                                c0 = (2 * k + jc) * P
                                last = nc.tensor.transpose(var_bank[0:C, c0:c0 + P], xn[o][:, s:s + C], identity)
                        last.then_inc(xnT_done, 1)
                    if ln2:
                        pe.wait_ge(xn2_ready, t)
                        wait(pe, xn_ready, last_quad(t + 2))
                        wait(pe, xc1_ready, last_quad(t + 2))
                        if not ln1:
                            wait(pe, logits_ready, t - 1)
                        for n in range(CHUNKS):
                            s = (n // 2) * N + START[n % 2]
                            last = nc.tensor.matmul(xc_bank[0:C, 2 * E * n:2 * E * n + 2 * E], xn2[:, s:s + C],
                                                    wr_block[:, :], start=True, stop=True)
                        last.then_inc(logits_done, 1)
                    if att:
                        weigh(1)
                    if late:
                        for part in range(len(EMBED)):
                            embedding(part)

                xt_now = None
                def banks_free():
                    pe.wait_ge(setup_vec, SETUP_ALL)

                steps(pe, step, {-1: set_up, 0: banks_free})

                def first_layer(u, p, e):
                    if e == 0:
                        pe.wait_ge(x2_hi_ready, 2 * u + 2)
                        pe.wait_ge(x2_lo_ready, 2 * u + 2)
                    for half in range(2):
                        bank = z1_bank[e % 2][half]
                        wait(pe, gelu_ready, 16 * u + 2 * e + half - 3)
                        nc.tensor.matmul(bank[:, 0:T], w1_hi[:, e, :], x2[p][half][:, :], start=True, stop=False)
                        nc.tensor.matmul(bank[:, 0:T], w1_lo[:, e, :], x2[p][half][:, :], start=False, stop=True)\
                            .then_inc(z1_done, 1)

                def spread_weights(u, p, e, has_next):
                    if e == 0:
                        pe.wait_ge(wT_ready, u + 1)
                    if e == TURN_WT + 1 and has_next:
                        pe.wait_ge(wT_ready, u + 2)
                    elif e == TURN_WT:
                        pe.wait_ge(wb_ready, 8 * u + e)
                    else:
                        wait(pe, wb_ready, 8 * u + e - 1)
                    nc.tensor.matmul(spread_bank[(p + turn(e)) % 2][:, 0:T], sel_r[:, e, :], wT[p][:, :],
                                     start=True, stop=True).then_inc(wb_done, 1)

                def second_layer(u, p, e):
                    pe.wait_ge(gelu_ready, 16 * u + 2 * e + 2)
                    wait(pe, weighted_ready, 8 * u + e - 1)
                    for half in range(2):
                        last = nc.tensor.matmul(y_bank[e % 2][D * half:D * half + D, 0:T], w2_sb[:, e, :],
                                                gelu[e % 4][half][:, :], start=True, stop=True)
                    last.then_inc(y_done, 1)

                def transpose_weights(u, p):
                    pe.wait_ge(w_lo_ready, u + 1)
                    wait(pe, wb_ready, 8 * (u - 1) + TURN_WT - 1)
                    bank = spread_bank[(1 - p + TURN_WT) % 2]
                    for n in range(CHUNKS):
                        s = (n // 2) * N + START[n % 2]
                        last = nc.tensor.transpose(bank[0:S, s:s + C], w_now[p][:, n, :, :, :].rearrange("p a h e -> p (a h e)"),
                                                   identity[0:C, 0:C])
                    last.then_inc(wT_done, 1)

                def quad(u, p, has_next, _):
                    for e in range(0, E, 2):
                        if e == TURN_WT and has_next:
                            transpose_weights(u + 1, 1 - p)
                        for d in range(2):
                            if e + 2 < E:
                                first_layer(u, p, e + 2 + d)
                            elif has_next:
                                first_layer(u + 1, 1 - p, d)
                            spread_weights(u, p, e + d, has_next)
                        for d in range(2):
                            second_layer(u, p, e + d)

                pe.wait_ge(logits_ready, NQ)
                pe.wait_ge(log2_ready, NQ)
                pe.wait_ge(exp_done, 4 * NQ)
                pe.wait_ge(h1_ready, NQ)
                pe.wait_ge(xc2_ready, NQ)
                pe.wait_ge(expert_weights_loaded, 16 * 4)
                transpose_weights(0, 0)
                first_layer(0, 0, 0)
                first_layer(0, 0, 1)
                quads(pe, quad)

            @block.scalar
            def _(act):
                act.preload_act_table_set("natural_log_exp_and_others")
                act.wait_ge(tok_w_loaded, 16 * 2)
                act.wait_ge(setup_vec, SETUP_COLUMNS)

                def step(t, p, has):
                    emb, ln1, att, ln2, choose = has
                    o = 1 - p

                    def exps(q, chunks=(0, 1)):
                        half = q % 2
                        if chunks[0] == 0:
                            act.wait_ge(nmax_ready, 4 * t + q + 1)
                            wait(act, pT_done, 4 * t + q - 1)
                        for c in chunks:
                            last = nc.scalar.activation(probs[half][:, c, :], s_bank[half][0:C, c * N:c * N + N],
                                                        ACT.Exp, bias=nmax[:, q, c:c + 1],
                                                        accum_out=psums[:, q, c:c + 1])
                        if c == 1:
                            last.then_inc(exp_done, 1)

                    def take_probsT(q):
                        act.wait_ge(pT_done, 4 * t + q + 1)
                        wait(act, pv_done, 2 * t + q // 2)
                        nc.scalar.copy(probsT[0][:, :, :], pT_bank[0][0:C, 0:T].rearrange("p (c n) -> p c n", c=2))\
                            .then_inc(pT_ready[0], 1)

                    if att:
                        exps(0)
                    if ln1:
                        act.wait_ge(xc1_done, t + 2)
                        wait(act, xn_ready, t + 1)
                        nc.scalar.activation(stat1[:, :], xc_bank[:, 0:T], ACT.Square)
                        nc.scalar.activation(sq1_hi[:, :], xc_bank[:, 0:T], ACT.Square).then_inc(sq1_ready, 1)
                    if att and not ln1:
                        exps(1)
                    if att and ln1:
                        exps(1, (0,))
                    if ln2:
                        act.wait_ge(var2_done, t)
                        nc.scalar.activation(stat2[:, :], var_bank[:, 0:T], ACT.Ln, bias=eps2[:, :], scale=1.0 + EPS)\
                            .then_inc(log2_ready, 1)
                    if att and ln1:
                        exps(1, (1,))
                    if ln1:
                        act.wait_ge(var1_done, t + 2)
                        nc.scalar.activation(stat1[:, :], var_bank[:, 0:T], ACT.Ln, bias=eps1[:, :])\
                            .then_inc(log1_ready, 1)
                    if ln1:
                        wait(act, xc2_ready, t)
                        nc.scalar.copy(xc1[o][:, :], xc_bank[:, 0:T]).then_inc(xc1_ready, 1)
                    if ln1:
                        act.wait_ge(log1_ready, t + 2)
                        nc.scalar.activation(stat1[:, :], stat1[:, :], ACT.Exp, scale=-0.5)\
                            .then_inc(rstd1_ready, 1)
                    if ln2:
                        act.wait_ge(log2_ready, t)
                        nc.scalar.activation(stat2[:, :], stat2[:, :], ACT.Exp, scale=-0.5)\
                            .then_inc(rstd2_ready, 1)
                    if att:
                        take_probsT(0)
                    if att:
                        exps(2)
                        exps(3)
                    if choose:
                        act.wait_ge(router_vec, VEC * (t - 2) + 12)
                        nc.scalar.activation(exp_gap[:, :, :], gap[:, :, :], ACT.Exp, scale=-1.0)\
                            .then_inc(exp_gap_ready, 1)
                    if att:
                        take_probsT(2)
                    if emb:
                        act.wait_ge(tok_done, t + 3)
                        wait(act, h_kept, t + 1)
                        nc.scalar.activation(h_hi[p][:, :].rearrange("p (k n) -> p k n", k=2)[:, :, 1:N],
                                             tok_bank[:, 0:2 * PATCHES].rearrange("p (k n) -> p k n", k=2),
                                             ACT.Identity, bias=tok_b).then_inc(h_hi_ready, 1)
                    if att:
                        act.wait_ge(xc2_ready, t + 1)
                        wait(act, xn2_ready, t)
                        nc.scalar.activation(stat2[:, :], xc2[:, :], ACT.Square)
                        nc.scalar.activation(sq2_hi[:, :], xc2[:, :], ACT.Square).then_inc(sq2_ready, 1)

                def split_hi(u, p):
                    act.wait_ge(xn2_kept, u + 1)
                    wait(act, z1_done, 16 * u - 16)
                    for half in range(2):
                        a, b = D * half, D * half + D
                        nc.scalar.copy(x2[p][half][a:b, :], xn2_store[a:b, u, :]).then_inc(x2_hi_ready, 1)

                def fetch_weights(u, p):
                    act.wait_ge(router_pool, POOL * u + POOL)
                    wait(act, wT_done, u - 1)
                    nc.scalar.copy(w_now[p][:, :, :, 0, :].bitcast(f32r), w_store[:, u, :, :, :]).then_inc(w_hi_ready, 1)

                def take_wT(u, p):
                    act.wait_ge(wT_done, u + 1)
                    wait(act, wb_done, 8 * u - 8)
                    nc.scalar.copy(wT[p][:, :], spread_bank[(1 - p + TURN_WT) % 2][0:S, 0:T]).then_inc(wT_ready, 1)

                def gelus(u, p, e):
                    for half in range(2):
                        act.wait_ge(z1_done, 16 * u + 2 * e + half + 1)
                        wait(act, y_done, 8 * u + e - 3)
                        nc.scalar.activation(gelu[e % 4][half][:, :], z1_bank[e % 2][half][:, 0:T], ACT.Gelu,
                                             bias=b1_full[:, e:e + 1]).then_inc(gelu_ready, 1)

                def take_wb(u, p, e):
                    act.wait_ge(wb_done, 8 * u + e + 1)
                    wait(act, weighted_ready, 8 * u + e - 1)
                    nc.scalar.copy(wb[e % 2][:, :], spread_bank[(p + turn(e)) % 2][:, 0:T]).then_inc(wb_ready, 1)

                def quad(u, p, has_next, has_after_next):
                    for e in range(E):
                        if e == TURN_WT and has_next:
                            take_wT(u + 1, 1 - p)
                        if e + 2 < E:
                            gelus(u, p, e + 2)
                        elif has_next:
                            gelus(u + 1, 1 - p, e + 2 - E)
                        take_wb(u, p, e)
                    if has_after_next:
                        split_hi(u + 2, p)
                        fetch_weights(u + 2, p)

                def first_quads():
                    for u in range(2):
                        split_hi(u, u)
                        fetch_weights(u, u)

                steps(act, step, {NQ: first_quads, NQ + 1: lambda: take_wT(0, 0)})
                act.preload_act_table_set("gelu_and_others")
                gelus(0, 0, 0)
                gelus(0, 0, 1)
                quads(act, quad)

            @block.vector
            def _(dve):
                count = [0]

                def wide(column):
                    return column[:, :, :].unsqueeze(3).to_broadcast(WIDE)

                def done(instruction):
                    count[0] += 1
                    instruction.then_inc(setup_vec, 1)
                    dve.wait_ge(setup_vec, count[0])

                done(nc.vector.memset(eps1[:, :], EPS))
                done(nc.vector.memset(eps2[:, :], EPS * EPS))
                done(nc.vector.memset(qk_block[:, :], 0.0))
                done(nc.vector.memset(wr_block[:, :], 0.0))
                dve.wait_ge(tok_w_loaded, 16 * 2)
                done(nc.vector.tensor_copy(beta_rows[:, :], beta[0:D, :].to_broadcast([D, C])))
                for p in range(2):
                    class_hi = h_hi[p][:, :].rearrange("p (k n) -> p k n", k=2)[:, :, 0]
                    done(nc.vector.tensor_copy(class_hi, cls_tok.to_broadcast([P, 2])))
                    done(nc.vector.tensor_tensor(h_lo[p][:, :].rearrange("p (k n) -> p k n", k=2)[:, :, 0],
                                                 cls_tok.to_broadcast([P, 2]), class_hi.bitcast(f32), ALU.subtract))
                assert count[0] == SETUP_COLUMNS

                def set_up_attention():
                    dve.wait_ge(weights_loaded, 16 * 7)
                    nc.vector.tensor_copy(center_r[:, :], center)
                    nc.vector.tensor_copy(mean_r[:, :], mean)
                    dve.wait_ge(setup_mm, 1)
                    for half in range(2):
                        a, b = D * half, D * half + D
                        done(nc.vector.tensor_scalar(qk_block[a:b, a:b], qk_bank[a:b, a:b], float(D) ** -0.5, None, ALU.mult))
                    assert count[0] == SETUP_ATTENTION

                def set_up_experts():
                    for half in range(2):
                        a, b = D * half, D * half + D
                        nc.vector.tensor_scalar(wr_block[a:b, half * E:half * E + E], wr_sb[a:b, :], gamma[a:b, :], None, ALU.mult)
                    nc.vector.tensor_tensor(br_full[0:C, :, :, :].rearrange("p c a e -> p (c a) e"),
                                            br_sb[0:C, :, :, :].rearrange("p c a e -> p (c a) e"),
                                            br_bank[0:C, 0:E].unsqueeze(1).to_broadcast([C, 2 * CHUNKS, E]), ALU.add)
                    dve.wait_ge(setup_mm, 2)
                    nc.vector.tensor_tensor(b1_full[:, :], b1_bank[:, 0:E], b1_sb[:, :], ALU.add)
                    done(nc.vector.tensor_scalar(w1_sb[:, :, :], w1_sb[:, :, :], gamma, None, ALU.mult))
                    done(nc.vector.tensor_copy(w1_hi[:, :, :], w1_sb[:, :, :]))
                    dve.wait_ge(expert_weights_loaded, 16 * 4)
                    nc.vector.tensor_copy(sel_r[:, :, :], sel_sb[:, :, :])
                    done(nc.vector.tensor_tensor(w1_lo[:, :, :], w1_sb[:, :, :], w1_hi[:, :, :].bitcast(f32), ALU.subtract))
                    assert count[0] == SETUP_ALL

                def step(t, p, has):
                    emb, ln1, att, ln2, choose = has
                    o = 1 - p

                    def maxima(q):
                        half = q % 2
                        dve.wait_ge(s_done, 4 * t + q + 1)
                        nc.vector.tensor_reduce(nmax[:, q, :], s_bank[half][0:C, 0:T].rearrange("p (c n) -> p c n", c=2),
                                                axis=AX.X, op=ALU.max, negate=True).then_inc(nmax_ready, 1)

                    def reciprocals(q):
                        dve.wait_ge(exp_done, 4 * t + q + 1)
                        nc.vector.reciprocal(rsums[:, q, :], psums[:, q, :]).then_inc(rsum_ready, 1)

                    def normalize(q):
                        dve.wait_ge(rsum_ready, 4 * t + q + 1)
                        for c in range(2):
                            last = nc.vector.tensor_scalar(probs[q % 2][:, c, :], probs[q % 2][:, c, :],
                                                           rsums[:, q, c:c + 1], None, ALU.mult)
                        last.then_inc(probs_ready[q % 2], 1)

                    def take_probsT(q):
                        dve.wait_ge(pT_done, 4 * t + q + 1)
                        wait(dve, pv_done, 2 * t + q // 2)
                        nc.vector.tensor_copy(probsT[1][:, :, :],
                                              pT_bank[1][0:C, 0:T].rearrange("p (c n) -> p c n", c=2))\
                            .then_inc(pT_ready[1], 1)

                    def choice(u, first_step, end):
                        for r in range(first_step, end):
                            if r == 0:
                                dve.wait_ge(logits_ready, u + 1)
                            elif r != 12:
                                dve.wait_ge(router_vec, VEC * u + r)
                            if r == 0:
                                step = nc.vector.tensor_reduce(top1[:, :, :], logits[:, :, :, :], axis=AX.X, op=ALU.max)
                            elif r == 1:
                                step = nc.vector.tensor_tensor(is_max[:, :, :, :], logits[:, :, :, :], wide(top1), ALU.is_equal)
                            elif r == 2:
                                step = nc.vector.tensor_tensor(ranked[:, :, :, :], is_max[:, :, :, :], prio[0:C, :, :, :], ALU.mult)
                            elif r == 3:
                                step = nc.vector.tensor_reduce(best[:, :, :], ranked[:, :, :, :], axis=AX.X, op=ALU.max)
                            elif r == 4:
                                wait(dve, router_pool, POOL * u)
                                step = nc.vector.tensor_tensor(first[:, :, :, :], ranked[:, :, :, :], wide(best), ALU.is_equal)
                            elif r == 5:
                                step = nc.vector.scalar_tensor_tensor(rest[:, :, :, :], first[:, :, :, :], -3.0e38,
                                                                      logits[:, :, :, :], ALU.mult, ALU.add)
                            elif r == 6:
                                step = nc.vector.tensor_reduce(top2[:, :, :], rest[:, :, :, :], axis=AX.X, op=ALU.max)
                            elif r == 7:
                                step = nc.vector.tensor_tensor(is_max[:, :, :, :], rest[:, :, :, :], wide(top2), ALU.is_equal)
                            elif r == 8:
                                step = nc.vector.tensor_tensor(ranked[:, :, :, :], is_max[:, :, :, :], prio[0:C, :, :, :], ALU.mult)
                            elif r == 9:
                                step = nc.vector.tensor_reduce(best[:, :, :], ranked[:, :, :, :], axis=AX.X, op=ALU.max)
                            elif r == 10:
                                step = nc.vector.tensor_tensor(second[:, :, :, :], ranked[:, :, :, :], wide(best), ALU.is_equal)
                            elif r == 11:
                                step = nc.vector.tensor_tensor(gap[:, :, :], top1[:, :, :], top2[:, :, :], ALU.subtract)
                            elif r == 12:
                                dve.wait_ge(exp_gap_ready, u + 1)
                                step = nc.vector.tensor_scalar(sum_exp[:, :, :], exp_gap[:, :, :], 1.0, None, ALU.add)
                            elif r == 13:
                                step = nc.vector.reciprocal(weight1[:, :, :], sum_exp[:, :, :])
                            elif r == 14:
                                step = nc.vector.tensor_tensor(weight2[:, :, :], exp_gap[:, :, :], weight1[:, :, :], ALU.mult)
                            step.then_inc(router_vec, 1)

                    def add_attention():
                        dve.wait_ge(h_kept, t)
                        nc.vector.tensor_tensor(h1_store[:, t - 1, :], pv_bank[:, 0:T], h1_store[:, t - 1, :], ALU.add)\
                            .then_inc(h1_ready, 1)

                    def normed_for_experts():
                        dve.wait_ge(rstd2_ready, t)
                        wait(dve, xn2_kept, t - 1)
                        wait(dve, logits_done, t - 1)
                        nc.vector.tensor_tensor(xn2[:, :], xc2[:, :], stat2[:, :], ALU.mult).then_inc(xn2_ready, 1)

                    if att:
                        maxima(0)
                        maxima(1)
                    if choose and not att:
                        choice(t - 2, 2, 6)
                    if ln2:
                        dve.wait_ge(sq2_ready, t)
                        nc.vector.tensor_tensor(sq2_lo[:, :], stat2[:, :], sq2_hi[:, :].bitcast(f32), ALU.subtract)\
                            .then_inc(sq2_lo_ready, 1)
                    if choose and att:
                        choice(t - 2, 2, 3)
                    if att:
                        reciprocals(0)
                        normalize(0)
                    if ln1:
                        dve.wait_ge(sq1_ready, t + 2)
                        nc.vector.tensor_tensor(sq1_lo[:, :], stat1[:, :], sq1_hi[:, :].bitcast(f32), ALU.subtract)\
                            .then_inc(sq1_lo_ready, 1)
                    if ln2 and ln1:
                        add_attention()
                    if choose and att:
                        choice(t - 2, 3, 4)
                    if att:
                        reciprocals(1)
                    if ln2 and not ln1:
                        add_attention()
                    if choose and not att:
                        choice(t - 2, 6, 12)
                    if ln2 and not att:
                        normed_for_experts()
                    if choose and att:
                        choice(t - 2, 4, 7)
                    if att:
                        maxima(2)
                    if ln1:
                        dve.wait_ge(rstd1_ready, t + 2)
                        nc.vector.tensor_tensor(xn[o][:, :], xc_bank[:, 0:T], stat1[:, :], ALU.mult)\
                            .then_inc(xn_ready, 1)
                    if att:
                        take_probsT(1)
                    if choose and att:
                        choice(t - 2, 7, 8)
                    if att:
                        maxima(3)
                    if choose and att:
                        choice(t - 2, 8, 9)
                    if att:
                        reciprocals(2)
                    if choose and att:
                        choice(t - 2, 9, 10)
                    if ln1:
                        dve.wait_ge(z_done, t + 2)
                        nc.vector.tensor_copy(z[o][:, :], var_bank[:, 0:T]).then_inc(z_ready, 1)
                    if choose and att:
                        choice(t - 2, 10, 11)
                    if att:
                        reciprocals(3)
                        normalize(3)
                    if choose and att:
                        choice(t - 2, 11, 12)
                    if ln2 and att:
                        normed_for_experts()
                    if choose and not att:
                        choice(t - 2, 12, 15)
                    if choose and att:
                        choice(t - 2, 12, 14)
                    if att:
                        take_probsT(3)
                    if choose and att:
                        choice(t - 2, 14, 15)
                    if ln1:
                        dve.wait_ge(xnT_done, t + 2)
                        nc.vector.tensor_copy(xnT[o][:, :, :, :],
                                              var_bank[0:C, :].rearrange("p (k j d) -> p k j d", k=2, j=2))\
                            .then_inc(xnT_ready, 1)
                    if ln2:
                        dve.wait_ge(logits_done, t)
                        nc.vector.tensor_tensor(logits[:, :, :, :],
                                                xc_bank[0:C, 0:2 * E * CHUNKS].rearrange("p (c a e) -> p c a e", a=2, e=E),
                                                br_full[0:C, :, :, :], ALU.add).then_inc(logits_ready, 1)
                    if isinstance(t, int) and t == -1:
                        set_up_experts()
                    if emb:
                        dve.wait_ge(h_hi_ready, t + 3)
                        wait(dve, h_kept, t + 1)
                        patches = lambda tile: tile.rearrange("p (k n) -> p k n", k=2)
                        nc.vector.scalar_tensor_tensor(patches(h_lo[p][:, :])[:, :, 1:N], patches(tok_bank[:, 0:2 * PATCHES]),
                                                       tok_b, patches(h_hi[p][:, :])[:, :, 1:N].bitcast(f32),
                                                       ALU.add, ALU.subtract).then_inc(h_lo_ready, 1)
                    if ln2:
                        choice(t - 1, 0, 1)
                    if att:
                        dve.wait_ge(pv_done, 2 * t + 2)
                        wait(dve, sq2_ready, t)
                        nc.vector.tensor_tensor(xc2[:, :], pv_bank[:, 0:T], xc1[p][:, :], ALU.add)\
                            .then_inc(xc2_ready, 1)
                    if ln2:
                        choice(t - 1, 1, 2)

                def weights_lo(u, p):
                    dve.wait_ge(w_hi_ready, u + 1)
                    nc.vector.tensor_tensor(w_now[p][:, :, :, 1, :], w_store[:, u, :, :, :], w_now[p][:, :, :, 0, :],
                                            ALU.subtract).then_inc(w_lo_ready, 1)

                def weigh_expert(u, p, e):
                    dve.wait_ge(y_done, 8 * u + e + 1)
                    dve.wait_ge(wb_ready, 8 * u + e + 1)
                    wait(dve, sum_ready, 8 * u + e - 1)
                    nc.vector.scalar_tensor_tensor(weighted[e % 2][:, :], y_bank[e % 2][:, 0:T], b2_sb[:, e:e + 1],
                                                   wb[e % 2][:, :], ALU.add, ALU.mult)\
                        .then_inc(weighted_ready, 1)

                def add_expert(u, p, e):
                    dve.wait_ge(weighted_ready, 8 * u + e + 1)
                    if e > 0:
                        dve.wait_ge(sum_ready, 8 * u + e)
                        base = result[p][:, :]
                    else:
                        if isinstance(u, int):
                            wait(dve, out_stored[p], 16 * (u // 2))
                        else:
                            dve.wait_ge(out_stored[p], 8 * (u - p))
                        dve.wait_ge(h1_ready, u + 1)
                        base = h1_store[:, u, :]
                    nc.vector.tensor_tensor(result[p][:, :], weighted[e % 2][:, :], base, ALU.add).then_inc(sum_ready, 1)

                def quad(u, p, has_next, _):
                    for e in range(E):
                        if e == 2 and has_next:
                            weights_lo(u + 1, 1 - p)
                        weigh_expert(u, p, e)
                        if e > 0:
                            add_expert(u, p, e - 1)
                        elif not (isinstance(u, int) and u == 0):
                            add_expert(u - 1, 1 - p, E - 1)

                steps(dve, step, {-1: set_up_attention, NQ + 1: lambda: weights_lo(0, 0)})
                quads(dve, quad)
                add_expert(NQ - 1, 1, E - 1)

            @block.gpsimd
            def _(pool):
                def wide(column):
                    return column[:, :, :].unsqueeze(3).to_broadcast(WIDE)

                def step(t, p, has):
                    emb, ln1, att, ln2, choose = has
                    def normalize(q):
                        half = q % 2
                        pool.wait_ge(rsum_ready, 4 * t + q + 1)
                        nc.gpsimd.tensor_tensor(probs[half][:, :, :], probs[half][:, :, :],
                                                rsums[:, q, :].unsqueeze(2).to_broadcast([C, 2, N]), ALU.mult)\
                            .then_inc(probs_ready[half], 1)

                    if ln1:
                        pool.wait_ge(h_hi_ready, t + 2)
                        pool.wait_ge(h_lo_ready, t + 2)
                        nc.gpsimd.tensor_tensor(h1_store[:, t + 1, :], h_hi[1 - p][:, :].bitcast(f32),
                                                h_lo[1 - p][:, :].bitcast(f32), ALU.add).then_inc(h_kept, 1)
                    if att:
                        normalize(1)
                    if att:
                        normalize(2)
                    if ln2:
                        pool.wait_ge(xn2_ready, t)
                        nc.gpsimd.tensor_copy(xn2_store[:, t - 1, :], xn2[:, :]).then_inc(xn2_kept, 1)
                    if choose:
                        b = POOL * (t - 2)
                        pool.wait_ge(router_vec, VEC * (t - 2) + VEC)
                        nc.gpsimd.tensor_tensor(part_a[:, :, :, :], first[:, :, :, :], wide(weight1), ALU.mult)\
                            .then_inc(router_pool, 1)
                        nc.gpsimd.tensor_tensor(part_b[:, :, :, :], second[:, :, :, :], wide(weight2), ALU.mult)\
                            .then_inc(router_pool, 1)
                        pool.wait_ge(router_pool, b + 2)
                        nc.gpsimd.tensor_tensor(w_store[:, t - 2, :, :, :], part_a[:, :, :, :], part_b[:, :, :, :], ALU.add)\
                            .then_inc(router_pool, 1)

                def split_lo(u, p):
                    for half in range(2):
                        a, b = D * half, D * half + D
                        c, d = D * (1 - half), D * (1 - half) + D
                        pool.wait_ge(xn2_kept, u + 1)
                        pool.wait_ge(x2_hi_ready, 2 * u + half + 1)
                        wait(pool, x2_lo_ready, 2 * u + half)
                        nc.gpsimd.tensor_tensor(x2[p][half][c:d, :], xn2_store[a:b, u, :],
                                                x2[p][half][a:b, :].bitcast(f32), ALU.subtract)\
                            .then_inc(x2_lo_ready, 1)

                def quad(u, p, has_next, has_after_next):
                    if has_after_next:
                        split_lo(u + 2, p)

                def first_quads():
                    pool.wait_ge(router_pool, POOL * (NQ - 2))
                    split_lo(0, 0)
                    split_lo(1, 1)
                    pool.wait_ge(x2_lo_ready, 4)

                steps(pool, step, {NQ: first_quads})
                pool.wait_ge(router_pool, POOL * NQ)
                quads(pool, quad)


SETUP_COLUMNS, SETUP_ATTENTION, SETUP_ALL = 9, 11, 14


def kernel(**inputs):
    import numpy as np
    import concourse.bacc as bacc
    from concourse import mybir
    from concourse.bass_utils import run_bass_kernel_spmd

    a = {k: np.asarray(v) for k, v in inputs.items()}
    PATCH, PARTS = 16, 128
    B, CH, H, W = a["x"].shape
    nh, nw = H // PATCH, W // PATCH
    D = a["L0_tok_W"].shape[0]
    E = a["L0_ffn_W1"].shape[0]
    NQ = B // 4
    rows = PARTS // PATCH
    chunks = PATCH // rows

    x = a["x"].reshape(NQ, 2, 2, CH, nh, chunks, rows, nw, PATCH).transpose(0, 6, 8, 3, 5, 1, 2, 4, 7)
    x = np.ascontiguousarray(x).reshape(NQ, PARTS, CH * chunks, 2, 2 * nh * nw)
    twice = lambda m: np.concatenate([m, m], axis=0)
    arrays = {
        "x": x,
        "tok_w": a["L0_tok_W"].T.reshape(CH * chunks, PARTS, D).transpose(1, 0, 2),
        "columns": twice(np.stack([a["L0_tok_b"], a["cls_tok"].reshape(D), a["L0_ffn_gamma"], a["L0_ffn_beta"]], axis=1)),
        "wq": a["L0_attn_Wq"],
        "wk": a["L0_attn_Wk"],
        "w1": twice(a["L0_ffn_W1"].transpose(1, 0, 2)),
        "b1": a["L0_ffn_b1"].T,
        "wr": twice(a["L0_ffn_Wr"]),
        "br": np.broadcast_to(a["L0_ffn_br"], (PARTS, 4, 2, E)),
        "w2": a["L0_ffn_W2"].transpose(1, 0, 2),
        "b2": twice(a["L0_ffn_b2"].T),
    }
    blocks = np.kron(np.eye(2), np.ones((D, D))) / D
    arrays["mats"] = np.stack([np.eye(PARTS) - blocks, blocks, np.eye(PARTS)], axis=1)
    rows_of = np.zeros((2, 2, E, E, 2, D))
    for half in range(2):
        rows_of[half, :, :, :, half, :] = np.eye(E)[:, :, None]
    arrays["selectors"] = rows_of.reshape(4 * E, E, PARTS)
    arrays["priority"] = np.broadcast_to(np.arange(E, 0, -1), (PARTS, 4, 2, E))

    nc = bacc.Bacc("TRN2", target_bir_lowering=False, num_devices=1)
    feeds, handles = {}, {}
    for name, value in arrays.items():
        feeds[name + "_in"] = np.ascontiguousarray(value, dtype=np.float32)
        handles[name] = nc.dram_tensor(name + "_in", value.shape, mybir.dt.float32, kind="ExternalInput").ap()
    N = nh * nw + 1
    out = nc.dram_tensor("tokens_out", (NQ, PARTS, 2 * N), mybir.dt.float32, kind="ExternalOutput").ap()
    vit_block_program(nc, out=out, **handles)
    got = run_bass_kernel_spmd(nc, [feeds], core_ids=[0]).results[0]["tokens_out"]
    return got.reshape(NQ, 2, D, 2, N).transpose(0, 1, 3, 4, 2).reshape(B, N, D)
```
